# Optimizing a Trainium2 kernel written in Bass

```python
import numpy as np
import jax
import jax.numpy as jnp

def _softmax(x, axis=-1):
    return jax.nn.softmax(x, axis=axis)

def _gelu(x):
    return jax.nn.gelu(x, approximate=True)

def _silu(x):
    return jax.nn.silu(x)

def _sigmoid(x):
    return jax.nn.sigmoid(x)

def _layernorm(x, axis=-1, eps=1e-05):
    m = jnp.mean(x, axis=axis, keepdims=True)
    v = jnp.var(x, axis=axis, keepdims=True)
    return (x - m) / jnp.sqrt(v + eps)

def _scatter_add(tgt, idx, src, axis=0):
    return tgt.at[idx].add(src)

def _segment_sum(src, seg, n):
    return jax.ops.segment_sum(src, seg, n)
kernel_name = 'mk_macaron_d1_jaxref_r4_7565a8'

def setup_inputs(seed: int=0):
    np.random.seed(seed)
    _w = jnp.asarray

    def _L0_attn_setup():
        import jax, jax.numpy as jnp
        import numpy as np
        B, T, C, H = (2, 512, 256, 16)
        key = jax.random.key(seed)
        ks = jax.random.split(key, 6)
        x = jax.random.normal(ks[0], (B, T, C), dtype=jnp.float32)
        wq = jax.random.normal(ks[1], (C, H * 3), dtype=jnp.float32) * C ** (-0.5)
        wk = jax.random.normal(ks[2], (C, H * 3), dtype=jnp.float32) * C ** (-0.5)
        wv = jax.random.normal(ks[3], (C, C), dtype=jnp.float32) * C ** (-0.5)
        wo = jax.random.normal(ks[4], (C, C), dtype=jnp.float32) * C ** (-0.5)
        dirs = jax.random.normal(ks[5], (H, 3), dtype=jnp.float32)
        head_dirs = dirs / jnp.linalg.norm(dirs, axis=1, keepdims=True)
        scale = jnp.full((1,), 1.0 / np.sqrt(3.0), dtype=jnp.float32)
        return {'x': x, 'wq': wq, 'wk': wk, 'wv': wv, 'wo': wo, 'head_dirs': head_dirs, 'scale': scale}
    _L0_attn_in = _L0_attn_setup()

    def _L0_ffn_setup():
        import jax, jax.numpy as jnp
        import numpy as np
        DIM = 256
        HIDDEN = 768
        SCALE = 1.0 / 127.0

        def _dequant(w_int, dtype):
            return w_int.astype(dtype) * jnp.asarray(SCALE, dtype)
        key = jax.random.key(seed)
        k_x, k_g, k_u, k_d = jax.random.split(key, 4)
        x = jax.random.normal(k_x, (4, 512, DIM), dtype=jnp.float32)
        w_gate = jax.random.randint(k_g, (HIDDEN, DIM), -127, 128, dtype=jnp.int32)
        w_up = jax.random.randint(k_u, (HIDDEN, DIM), -127, 128, dtype=jnp.int32)
        w_down = jax.random.randint(k_d, (DIM, HIDDEN), -127, 128, dtype=jnp.int32)
        return {'x': x, 'w_gate': w_gate, 'w_up': w_up, 'w_down': w_down}
    _L0_ffn_in = _L0_ffn_setup()
    _d = {'L0_attn_x': _L0_attn_in['x'], 'L0_attn_wq': _L0_attn_in['wq'], 'L0_attn_wk': _L0_attn_in['wk'], 'L0_attn_wv': _L0_attn_in['wv'], 'L0_attn_wo': _L0_attn_in['wo'], 'L0_attn_head_dirs': _L0_attn_in['head_dirs'], 'L0_attn_scale': _L0_attn_in['scale'], 'L0_ffn_w_gate': _L0_ffn_in['w_gate'], 'L0_ffn_w_up': _L0_ffn_in['w_up'], 'L0_ffn_w_down': _L0_ffn_in['w_down']}
    _x0 = _d['L0_attn_x']
    _d['L0_attn_x'] = jax.random.normal(jax.random.fold_in(jax.random.key(seed), 1), (8, 1024, 256), dtype=_x0.dtype)
    del _x0
    return _d

def reference(L0_attn_x, L0_attn_wq, L0_attn_wk, L0_attn_wv, L0_attn_wo, L0_attn_head_dirs, L0_attn_scale, L0_ffn_w_gate, L0_ffn_w_up, L0_ffn_w_down):

    def _L0_attn_ref(x, wq, wk, wv, wo, head_dirs, scale):
        import jax, jax.numpy as jnp
        import numpy as np
        B, T, C, H = (2, 512, 256, 16)
        b, t, c = x.shape
        h = head_dirs.shape[0]
        hd = c // h
        q3 = (x @ wq).reshape(b, t, h, 3).transpose(0, 2, 1, 3)
        k3 = (x @ wk).reshape(b, t, h, 3).transpose(0, 2, 1, 3)
        v = (x @ wv).reshape(b, t, h, hd).transpose(0, 2, 1, 3)
        q_on_dir = jnp.einsum('bhtd,hd->bht', q3, head_dirs)
        k_on_dir = jnp.einsum('bhtd,hd->bht', k3, head_dirs)
        dot_scores = jnp.einsum('bhtd,bhsd->bhts', q3, k3) * scale
        geo_bias = q_on_dir[..., :, None] * k_on_dir[..., None, :]
        scores = dot_scores + geo_bias
        causal = jnp.tril(jnp.ones((t, t), dtype=bool))
        scores = jnp.where(causal, scores, -jnp.inf)
        attn = jax.nn.softmax(scores, axis=-1)
        out = jnp.einsum('bhts,bhsd->bhtd', attn, v)
        out = out.transpose(0, 2, 1, 3).reshape(b, t, c)
        return out @ wo

    def _L0_ffn_ref(x, w_gate, w_up, w_down):
        import jax, jax.numpy as jnp
        import numpy as np
        DIM = 256
        HIDDEN = 768
        SCALE = 1.0 / 127.0

        def _dequant(w_int, dtype):
            return w_int.astype(dtype) * jnp.asarray(SCALE, dtype)
        wg = _dequant(w_gate, x.dtype)
        wu = _dequant(w_up, x.dtype)
        wd = _dequant(w_down, x.dtype)
        gate = jnp.einsum('bsd,hd->bsh', x, wg)
        up = jnp.einsum('bsd,hd->bsh', x, wu)
        h = jax.nn.silu(gate) * up
        return jnp.einsum('bsh,dh->bsd', h, wd)
    x = L0_attn_x
    x = x + 0.5 * _L0_ffn_ref(_layernorm(x, axis=-1), L0_ffn_w_gate, L0_ffn_w_up, L0_ffn_w_down)
    x = x + _L0_attn_ref(_layernorm(x, axis=-1), L0_attn_wq, L0_attn_wk, L0_attn_wv, L0_attn_wo, L0_attn_head_dirs, L0_attn_scale)
    x = x + 0.5 * _L0_ffn_ref(_layernorm(x, axis=-1), L0_ffn_w_gate, L0_ffn_w_up, L0_ffn_w_down)
    return x

_drawn_inputs = setup_inputs


def setup_inputs(seed=0):
    import zlib

    import numpy as np

    out = dict(_drawn_inputs(seed))
    spreads = {}
    factors = {'L0_attn_wq': 8.0,
     'L0_attn_wk': 8.0,
     'L0_attn_wv': 8.0,
     'L0_attn_wo': 8.0,
     'L0_attn_head_dirs': 8.0}
    for name, (base, spread) in spreads.items():
        noise = np.random.default_rng([zlib.crc32(name.encode()), seed]).standard_normal(out[name].shape)
        drawn = base * np.exp(spread * noise) if base else spread * noise
        out[name] = jnp.asarray(drawn.astype(out[name].dtype))
    for name, factor in factors.items():
        out[name] = (out[name] * factor).astype(out[name].dtype)
    return out
```

```python
from contextlib import ExitStack

import concourse.bass as bass
from concourse import mybir

F32 = mybir.dt.float32
F32R = mybir.dt.float32r
BF16 = mybir.dt.bfloat16
I32 = mybir.dt.int32
ALU = mybir.AluOpType
ACT = mybir.ActivationFunctionType
AX_X = mybir.AxisListType.X

P = 128
CHUNK = 512
TPC = CHUNK // P
EPS = 1e-5
W_SCALE = 1.0 / 127.0
MASKED = -1.0e30


class Buffers:
    pass


def ffn_stage(nc, ctx, g, tag, w_gate, w_up, w_down, x_in, x_out):
    C = w_gate.shape[0]
    HID = w_gate.shape[1]
    KC = C // P
    MH = HID // P
    T = g.x.shape[1]
    NCH = T // TPC
    TANH_SCALE = 0.5 * W_SCALE
    OUT_SCALE = 0.5 * 0.5 * W_SCALE * W_SCALE * W_SCALE
    x = g.x

    def sb(name, shape, dt):
        return ctx.enter_context(nc.sbuf_tensor(f"{tag}_{name}", shape, dt))

    def sem(name):
        return ctx.enter_context(nc.semaphore(f"{tag}_{name}"))

    w_hi = sb("w_hi", [P, 3 * KC * HID], F32R)
    w_lo = sb("w_lo", [P, 3 * KC * HID], F32R)
    NW = KC * HID

    def view(w, n):
        k = KC if n < 2 else MH
        return w[:, n * NW:(n + 1) * NW].rearrange("p (k n) -> p k n", k=k)

    flag = sb("flag", [1, 1], I32)
    with ExitStack() as prep:
        w_int = prep.enter_context(nc.sbuf_tensor(f"{tag}_w_int", [P, 3 * NW], I32))
        w_f32 = prep.enter_context(nc.sbuf_tensor(f"{tag}_w_f32", [P, 3 * NW], F32))
        lo_max = prep.enter_context(nc.sbuf_tensor(f"{tag}_lo_max", [P, 3], F32))
        flag_ps = prep.enter_context(nc.psum_tensor(f"{tag}_flag_ps", [1, 512], F32))
        int_loaded = [sem(f"int_loaded{n}") for n in range(3)]
        f32_done = sem("f32_done")
        hi_done = sem("hi_done")
        lo_done = sem("lo_done")
        max_done = sem("max_done")
        sum_done = sem("sum_done")
        flag_done = sem("flag_done")
        parts = [slice(n * NW, (n + 1) * NW) for n in range(3)]
        block = prep.enter_context(nc.Block())

        @block.sync
        def _(sp):
            for n, w in enumerate((w_gate, w_up, w_down)):
                sp.dma_start(w_int[:, parts[n]].rearrange("p (k n) -> p k n", k=w.shape[0] // P),
                             w.rearrange("(k p) n -> p k n", p=P)).then_inc(int_loaded[n], 16)

        @block.scalar
        def _(act):
            for n in range(3):
                act.wait_ge(int_loaded[n], 16)
                nc.scalar.copy(w_f32[:, parts[n]], w_int[:, parts[n]]).then_inc(f32_done, 1)

        @block.vector
        def _(dve):
            for n in range(3):
                dve.wait_ge(f32_done, n + 1)
                nc.vector.tensor_copy(w_hi[:, parts[n]], w_f32[:, parts[n]]).then_inc(hi_done, 1)
                dve.wait_ge(hi_done, n + 1)
                nc.vector.tensor_tensor(w_lo[:, parts[n]], w_f32[:, parts[n]], w_hi[:, parts[n]],
                                        ALU.subtract).then_inc(lo_done, 1)
                dve.wait_ge(lo_done, n + 1)
                nc.vector.tensor_reduce(lo_max[:, n:n + 1], w_lo[:, parts[n]], AX_X, ALU.max,
                                        apply_absolute_value=True).then_inc(max_done, 1)
            dve.wait_ge(sum_done, 1)
            nc.vector.tensor_reduce(flag[:, :], flag_ps[:, 0:3], AX_X, ALU.max).then_inc(flag_done, 1)

        @block.tensor
        def _(pe):
            pe.wait_ge(max_done, 3)
            pe.wait_ge(g.consts_done, g.N_CONSTS)
            nc.tensor.matmul(flag_ps[:, 0:3], g.ones[:, 0:1], lo_max[:, :],
                             start=True, stop=True).then_inc(sum_done, 1)

    xn = sb("xn", [P, 2, TPC, C], F32)
    x_hi = sb("x_hi", [P, 2, KC, CHUNK], F32R)
    x_lo = sb("x_lo", [P, 2, KC, CHUNK], F32R)
    h_hi = sb("h_hi", [P, 2, MH, CHUNK], F32R)
    h_lo = sb("h_lo", [P, 2, MH, CHUNK], F32R)
    tanh_sb = sb("tanh_sb", [P, 2, CHUNK], F32)
    act_sb = sb("act_sb", [P, 2, CHUNK], F32)
    h_sb = sb("h_sb", [P, 3, CHUNK], F32)
    stats = sb("stats", [P, TPC, 6], F32)
    mv = sb("mv", [P, TPC, 2], F32)
    var_eps = sb("var_eps", [P, TPC], F32)
    rstd = sb("rstd", [P, TPC], F32)
    gate_up = ctx.enter_context(nc.psum_tensor(f"{tag}_gate_up", [P, 2, 2, CHUNK], F32))
    xt_ps = ctx.enter_context(nc.psum_tensor(f"{tag}_xt_ps", [P, KC, CHUNK], F32))
    y_ps = ctx.enter_context(nc.psum_tensor(f"{tag}_y_ps", [P, TPC // 2, 2, C], F32))

    x_loaded = [sem(f"x_loaded{p}") for p in range(2)]
    stats_done = sem("stats_done")
    mv_done = sem("mv_done")
    vareps_done = sem("vareps_done")
    rstd_done = sem("rstd_done")
    xn_done = sem("xn_done")
    xt_done = sem("xt_done")
    xhi_done = sem("xhi_done")
    xlo_done = sem("xlo_done")
    gate_done = sem("gate_done")
    up_done = sem("up_done")
    tanh_done = sem("tanh_done")
    act_done = sem("act_done")
    h_done = sem("h_done")
    hhi_done = sem("hhi_done")
    hlo_done = sem("hlo_done")
    y_done = sem("y_done")
    x_done = sem("x_done")
    x_stored = [sem(f"x_stored{p}") for p in range(2)]

    def chunks(eng, step):
        step(0, 0, True, False)
        step(1, 1, False, False)
        with eng.Fori(1, NCH // 2 - 1) as k:
            c2 = eng.snap(k * 2)
            step(c2, 0, False, False)
            step(c2 + 1, 1, False, False)
        step(NCH - 2, 0, False, False)
        step(NCH - 1, 1, False, True)

    block = ctx.enter_context(nc.Block())

    def tiles(c):
        return x[:, bass.ds(c * TPC, TPC), :]

    def half(c, n):
        return x[:, bass.ds(c * TPC + 2 * n, 2), :]

    @block.sync
    def _(sp):
        def load(c, p, first, last):
            if not first and not (isinstance(c, int) and c == 1):
                sp.wait_ge(x_loaded[p], (c - p) * 8)
            sp.dma_start(tiles(c), x_in[:, bass.ds(c * TPC, TPC), :]).then_inc(x_loaded[p], 16)

        def store(c, p, first, last):
            sp.wait_ge(x_done, (c + 1) * 2)
            sp.dma_start(x_out[:, bass.ds(c * TPC, TPC), :], tiles(c)).then_inc(x_stored[p], 16)

        if x_in is not None:
            chunks(sp, load)
        if x_out is not None:
            chunks(sp, store)
            for p in range(2):
                sp.wait_ge(x_stored[p], NCH // 2 * 16)

    @block.gpsimd
    def _(pool):
        def rstd_of(c):
            pool.wait_ge(mv_done, c + 1)
            nc.gpsimd.tensor_tensor(var_eps[:, :], mv[:, :, 1], g.eps[:, 0:TPC], ALU.add).then_inc(vareps_done, 1)
            pool.wait_ge(vareps_done, c + 1)
            nc.gpsimd.tensor_tensor(rstd[:, :], var_eps[:, :], g.neg_half[:, 0:TPC],
                                    ALU.pow).then_inc(rstd_done, 1)

        def step(c, p, first, last):
            if not last:
                rstd_of(c + 1)
            for m in range(MH):
                n = c * MH + m
                pool.wait_ge(h_done, n + 1)
                pool.wait_ge(hhi_done, n + 1)
                if not first and not (isinstance(c, int) and c == 1):
                    pool.wait_ge(y_done, (c - 1) * 2)
                nc.gpsimd.tensor_tensor(h_lo[:, p, m, :], h_sb[:, m % 3, :], h_hi[:, p, m, :],
                                        ALU.subtract).then_inc(hlo_done, 1)

        pool.wait_ge(g.consts_done, g.N_CONSTS)
        rstd_of(0)
        chunks(pool, step)

    @block.scalar
    def _(act):
        def split_x(c, p):
            for kc in range(KC):
                act.wait_ge(xt_done, c * KC + kc + 1)
                nc.scalar.copy(x_hi[:, p, kc, :], xt_ps[:, kc, :]).then_inc(xhi_done, 1)

        def step(c, p, first, last):
            def h_high(m):
                n = c * MH + m
                act.wait_ge(h_done, n + 1)
                if not first and not (isinstance(c, int) and c == 1):
                    act.wait_ge(y_done, (c - 1) * 2)
                nc.scalar.copy(h_hi[:, p, m, :], h_sb[:, m % 3, :]).then_inc(hhi_done, 1)

            for m in range(MH):
                n = c * MH + m
                act.wait_ge(gate_done, n + 1)
                if not (first and m < 2):
                    act.wait_ge(act_done, n - 1)
                nc.scalar.activation(tanh_sb[:, m % 2, :], gate_up[:, m % 2, 0, :], ACT.Tanh,
                                     scale=TANH_SCALE).then_inc(tanh_done, 1)
                if m >= 1:
                    h_high(m - 1)
                if m == 4 and not last:
                    split_x(c + 1, 1 - p)
            h_high(MH - 1)

        split_x(0, 0)
        chunks(act, step)

    @block.vector
    def _(dve):
        def ln_stats(c, p):
            if x_in is not None:
                dve.wait_ge(x_loaded[p], (c - p) * 8 + 16)
            for i in range(TPC):
                last = nc.vector.bn_stats(stats[:, i, :], x[:, bass.ds(c * TPC + i, 1), :].rearrange("p a c -> p (a c)"))
            last.then_inc(stats_done, 1)

        def ln_gather():
            for i in range(TPC):
                last = nc.vector.bn_aggr(mv[:, i, :], stats[:, i, :])
            last.then_inc(mv_done, 1)

        def ln_norm(c, p):
            dve.wait_ge(rstd_done, c + 1)
            if not (isinstance(c, int) and c < 2):
                dve.wait_ge(xt_done, (c - 1) * KC)
            for i in range(TPC):
                last = nc.vector.tensor_scalar(xn[:, p, i, :], x[:, bass.ds(c * TPC + i, 1), :].rearrange("p a c -> p (a c)"),
                                               mv[:, i, 0:1], rstd[:, i:i + 1], ALU.subtract, ALU.mult)
            last.then_inc(xn_done, 1)

        def split_x(c, p):
            for kc in range(KC):
                dve.wait_ge(xhi_done, c * KC + kc + 1)
                nc.vector.tensor_tensor(x_lo[:, p, kc, :], xt_ps[:, kc, :], x_hi[:, p, kc, :],
                                        ALU.subtract).then_inc(xlo_done, 1)

        def residual(c, n):
            dve.wait_ge(y_done, c * 2 + n + 1)
            nc.vector.scalar_tensor_tensor(out=half(c, n), in0=y_ps[:, n, :, :], scalar=OUT_SCALE,
                                           in1=half(c, n), op0=ALU.mult, op1=ALU.add).then_inc(x_done, 1)

        def step(c, p, first, last):
            def gate(m):
                n = c * MH + m
                dve.wait_ge(tanh_done, n + 1)
                nc.vector.scalar_tensor_tensor(out=act_sb[:, m % 2, :], in0=tanh_sb[:, m % 2, :], scalar=1.0,
                                               in1=gate_up[:, m % 2, 0, :], op0=ALU.add,
                                               op1=ALU.mult).then_inc(act_done, 1)

            def up(m):
                n = c * MH + m
                dve.wait_ge(act_done, n + 1)
                dve.wait_ge(up_done, n + 1)
                if not (first and m < 3):
                    dve.wait_ge(hlo_done, n - 2)
                nc.vector.tensor_tensor(h_sb[:, m % 3, :], act_sb[:, m % 2, :], gate_up[:, m % 2, 1, :],
                                        ALU.mult).then_inc(h_done, 1)

            for m in range(MH):
                if m == 0 and not last:
                    ln_stats(c + 1, 1 - p)
                    dve.wait_ge(stats_done, c + 2)
                    dve.wait_ge(xn_done, c + 1)
                gate(m)
                if m == 0 and not last:
                    ln_gather()
                if m == 2 and not last:
                    ln_norm(c + 1, 1 - p)
                up(m)
                if m in (3, 4) and not first:
                    residual(c - 1, m - 3)
                if m == 4 and not last:
                    split_x(c + 1, 1 - p)

        ln_stats(0, 0)
        dve.wait_ge(stats_done, 1)
        ln_gather()
        ln_norm(0, 0)
        split_x(0, 0)
        dve.wait_ge(flag_done, 1)
        chunks(dve, step)
        residual(NCH - 1, 0)
        residual(NCH - 1, 1)

    @block.tensor
    def _(pe):
        def transpose_x(c, p):
            pe.wait_ge(xn_done, c + 1)
            if not (isinstance(c, int) and c == 0):
                pe.wait_ge(xlo_done, c * KC)
            for kc in range(KC):
                for i in range(TPC):
                    last = nc.tensor.transpose(xt_ps[:, kc, i * P:(i + 1) * P],
                                               xn[:, p, i, kc * P:(kc + 1) * P], g.ident[:, :])
                last.then_inc(xt_done, 1)

        def products(w, n, m, moving_hi, moving_lo, exact):
            for kc in range(KC):
                s = slice(m * P, (m + 1) * P)
                yield view(w_hi, n)[:, kc, s], moving_hi[:, kc, :]
                yield view(w_hi, n)[:, kc, s], moving_lo[:, kc, :]
                if not exact:
                    yield view(w_lo, n)[:, kc, s], moving_hi[:, kc, :]
                    yield view(w_lo, n)[:, kc, s], moving_lo[:, kc, :]

        def stage(exact):
            def down(c, p, i):
                if i == 0:
                    pe.wait_ge(hlo_done, (c + 1) * MH)
                if i % 2 == 0 and not (isinstance(c, int) and c == 0):
                    pe.wait_ge(x_done, c * 2 - 1 + i // 2)
                ops = []
                for m in range(MH):
                    s = slice(i * P, (i + 1) * P)
                    ops.append((h_hi[:, p, m, s], view(w_hi, 2)[:, m, :]))
                    ops.append((h_lo[:, p, m, s], view(w_hi, 2)[:, m, :]))
                    if not exact:
                        ops.append((h_hi[:, p, m, s], view(w_lo, 2)[:, m, :]))
                        ops.append((h_lo[:, p, m, s], view(w_lo, 2)[:, m, :]))
                for k, (stationary, moving) in enumerate(ops):
                    last = nc.tensor.matmul(y_ps[:, i // 2, i % 2, :], stationary, moving,
                                            start=(k == 0), stop=(k == len(ops) - 1))
                if i % 2:
                    last.then_inc(y_done, 1)

            def step(c, p, first, last):
                pe.wait_ge(xlo_done, (c + 1) * KC)
                for m in range(MH):
                    n = c * MH + m
                    if not (first and m < 2):
                        pe.wait_ge(h_done, n - 1)
                    for which, done in ((0, gate_done), (1, up_done)):
                        ops = list(products(w_hi, which, m, x_hi[:, p], x_lo[:, p], exact))
                        for k, (stationary, moving) in enumerate(ops):
                            last_mm = nc.tensor.matmul(gate_up[:, m % 2, which, :], stationary, moving,
                                                       start=(k == 0), stop=(k == len(ops) - 1))
                        last_mm.then_inc(done, 1)
                    if m == 3 and not last:
                        transpose_x(c + 1, 1 - p)
                    if not first and m in (1, 2, 3, 4):
                        down(c - 1, 1 - p, m - 1)

            chunks(pe, step)
            for i in range(TPC):
                down(NCH - 1, 1, i)

        pe.wait_ge(g.consts_done, g.N_CONSTS)
        transpose_x(0, 0)
        pe.wait_ge(flag_done, 1)
        has_low = pe.value_load(flag[0:1, 0:1], min_val=0, max_val=1 << 30)
        with pe.If(has_low > 0):
            stage(exact=False)
        with pe.Else():
            stage(exact=True)
        pe.nop()


HPG = 4
ROWS = 32
HD3 = 3
PARTS = ((0, 0), (0, 1), (1, 0), (1, 1))
ROW_MAX = HD3 * len(PARTS)


def attention_plan(NT, NG):
    per = CHUNK // P
    exp_units = []
    for tc in range(NT // per):
        for k in range((tc + 1) * per):
            off = max(0, k - tc * per) * P
            exp_units.append((tc, k, off, CHUNK - off))
    max_units = []
    for i in range(NT):
        if (i + 1) * P <= CHUNK:
            max_units += [(i, (0, 1)), (i, (2, 3))]
        else:
            max_units += [(i, (j,)) for j in range(HPG)]
    cost_e = [60 * HPG + HPG * n for _, _, _, n in exp_units]
    cost_m = [65 + len(js) * (i + 1) * P for i, js in max_units]
    first_half = 2 * len([1 for i, _ in max_units if i < per]) // 2

    def maxima(db, g):
        at, done, halves = 0, 0.0, [[] for _ in range(2 * len(exp_units))]
        spent, total_e, total_m = 0.0, sum(cost_e), sum(cost_m)
        for u, c in enumerate(cost_e):
            for half in range(2):
                spent += c / 2
                while at < len(max_units) and done / total_m <= spent / total_e - 1e-9:
                    halves[2 * u + half].append(("max", db, g, at))
                    done += cost_m[at]
                    at += 1
                    if at == first_half:
                        halves[2 * u + half].append(("MM", db, g, 0))
                        mt_at.append(u + 1)
        halves[-1] += [("max", db, g, n) for n in range(at, len(max_units))]
        halves[-1].append(("MM", db, g, 1))
        return halves

    mt_at = []

    def group(n):
        return n // NG, n % NG

    def misc(s, first, last):
        at = {}

        def put(slot, *events):
            at.setdefault(slot, []).extend(events)

        if not (last and s == NG - 1):
            put(0, ("LQ", *group(s + 1), 1))
        put(0, ("MT", 0, s, 1), ("NM", 0, s, 1))
        if not (last and s >= NG - 2):
            put(5, ("LQ", *group(s + 2), 0))
        if s == 0:
            if not last:
                put(5, ("STAT", 1, 0), ("AGGR", 1, 0))
                put(7, ("NORM", 1, 0))
                put(8, ("XT", 1, 0))
                put(9, ("STAT", 1, 1), ("AGGR", 1, 1))
                put(11, ("NORM", 1, 1))
            if not first:
                put(4, ("VA", 0, NG - 1))
                put(2, ("OT", -1, 2))
                put(3, ("AT", -1, 2))
                put(4, ("WO", -1, 2), ("OT", -1, 3))
                put(5, ("AT", -1, 3))
                put(6, ("WO", -1, 3))
                put(0, ("LK", 0, NG - 1))
        if not last:
            if s == 1:
                put(2, ("QK", 1, 0))
                put(3, ("V", 1, 0))
                put(5, ("XT", 1, 1))
                put(7, ("QK", 1, 1), ("SAVE", 1))
                put(9, ("V", 1, 1))
            if s == 2:
                put(0, ("LK", 1, 0), ("LK", 1, 1))
            if s == 3:
                put(2, ("LK", 1, 2))
                put(4, ("VA", 1, 0))
                put(5, ("VA", 1, 1))
                put(6, ("VA", 1, 2))
        if s == 3:
            put(6, ("OT", 0, 0))
            put(7, ("AT", 0, 0))
            put(8, ("WO", 0, 0), ("OT", 0, 1))
            put(9, ("AT", 0, 1))
            put(10, ("WO", 0, 1))
        return at

    def stage(s, first, last):
        events, at = [], misc(s, first, last)
        nxt = group(s + 1)
        if not (last and s == NG - 1):
            mt_at.clear()
            halves = maxima(*nxt)
            at.setdefault(mt_at[0] + 1, []).extend([("MT", *nxt, 0), ("NM", *nxt, 0)])
        else:
            halves = [[] for _ in range(2 * len(exp_units))]
        before = group(s - 1)
        for u in range(len(exp_units)):
            events += [("S", 0, s, u, 0), ("S", 0, s, u, 1)]
            events += halves[2 * u]
            events += [("S", 0, s, u, 2), ("S", 0, s, u, 3)]
            events += halves[2 * u + 1]
            if u:
                events.append(("PV", 0, s, u - 1))
                if u == per:
                    events.append(("O", 0, s, 0))
            elif not (first and s == 0):
                events += [("PV", *before, len(exp_units) - 1), ("O", *before, 1)]
            events += at.get(u, [])
        return events

    def body(first=False, last=False):
        return [e for s in range(NG) for e in stage(s, first, last)]

    prologue = []
    for h in range(2):
        prologue += [("STAT", 1, h), ("AGGR", 1, h), ("NORM", 1, h), ("XT", 1, h), ("QK", 1, h), ("V", 1, h)]
    prologue += [("SAVE", 1), ("LK", 1, 0), ("LQ", 1, 0, 0), ("LQ", 1, 0, 1), ("LQ", 1, 1, 0)]
    prologue += [("LK", 1, g) for g in range(1, NG)] + [("VA", 1, g) for g in range(NG)]
    prologue += [("max", 1, 0, n) for n in range(first_half)]
    prologue += [("MM", 1, 0, 0), ("MT", 1, 0, 0), ("NM", 1, 0, 0)]
    prologue += [("max", 1, 0, n) for n in range(first_half, len(max_units))] + [("MM", 1, 0, 1)]
    epilogue = [("PV", 0, NG - 1, len(exp_units) - 1), ("O", 0, NG - 1, 1)]
    for q in (2, 3):
        epilogue += [("OT", 0, q), ("AT", 0, q), ("WO", 0, q)]
    sections = [prologue, body(first=True), body(), body(last=True) + epilogue]

    ring, n, out = ("max", "MT", "XT", "QK", "V", "OT", "AT", "WO"), 0, []
    for at, section in enumerate(sections):
        uses = [e for e in section if e[0] in ring]
        if at == 2:
            assert len(uses) % 2 == 0
        before = [] if at == 0 else [(e[0], e[1] - 1, *e[2:]) for e in sections[at - 1] if e[0] in ring][-2:]
        known, placed = before + uses, []
        shift = len(before)
        for e in section:
            slot = held_by = None
            if e[0] in ring:
                slot = n % 2
                if shift >= 2:
                    held_by = known[shift - 2]
                n += 1
                shift += 1
            placed.append((e, slot, held_by))
        out.append(placed)
    return exp_units, max_units, out


def attention_stage(nc, ctx, g_, wq, wk, wv, wo, head_dirs, scale, B):
    x = g_.x
    C = wv.shape[0]
    KC = C // P
    H = head_dirs.shape[0]
    HD = C // H
    NG = H // HPG
    T = x.shape[1]
    NT = T // B
    SEQ = NT * P
    NTC = SEQ // CHUNK
    QKW = H * HD3
    K0 = 64
    exp_units, max_units, sections = attention_plan(NT, NG)
    NE, NM = len(exp_units), len(max_units)
    first_half = len([1 for i, _ in max_units if i < TPC])

    def sb(name, shape, dt):
        return ctx.enter_context(nc.sbuf_tensor(f"at_{name}", shape, dt))

    def sem(name):
        return ctx.enter_context(nc.semaphore(f"at_{name}"))

    w_qk = sb("w_qk", [P, KC, P], F32)
    w_v = sb("w_v", [P, KC, C], F32)
    w_o = sb("w_o", [P, KC, C], F32)
    ident_bf = sb("ident_bf", [P, P], BF16)
    future = sb("future", [P, P], BF16)
    past = sb("past", [P, P], BF16)
    q_rows = sb("q_rows", [P, 2, HPG, SEQ], F32R)
    k_rows = sb("k_rows", [P, NG, SEQ], F32R)
    q_dram = nc.dram_tensor("q_rows_dram", [B, H, ROW_MAX + 2, SEQ], F32).ap()
    k_dram = nc.dram_tensor("k_rows_dram", [B, H, ROW_MAX, SEQ], F32).ap()
    v_aug = sb("v_aug", [P, NT, H, 2 * HD], F32)
    neg_max = sb("neg_max", [P, TPC, P], F32)

    with ExitStack() as prep:
        dirs = prep.enter_context(nc.sbuf_tensor("at_dirs", [P, QKW], F32))
        scale_b = prep.enter_context(nc.sbuf_tensor("at_scale", [P, 1], F32))
        wk_sb = prep.enter_context(nc.sbuf_tensor("at_wk", [P, KC, QKW], F32))
        on_dir = prep.enter_context(nc.sbuf_tensor("at_on_dir", [P, KC, QKW], F32))
        on_dir_sum = prep.enter_context(nc.sbuf_tensor("at_on_dir_sum", [P, KC, H], F32))
        along = prep.enter_context(nc.sbuf_tensor("at_along", [P, KC, QKW], F32))
        qk_cleared = prep.enter_context(nc.semaphore("at_qk_cleared"))
        future_cleared = prep.enter_context(nc.semaphore("at_future_cleared"))
        loaded = prep.enter_context(nc.semaphore("at_loaded"))
        fold = prep.enter_context(nc.semaphore("at_fold"))
        zeros = prep.enter_context(nc.sbuf_tensor("at_zeros", [P, 2, SEQ], F32))
        zeros_done = prep.enter_context(nc.semaphore("at_zeros_done"))
        zeroed = prep.enter_context(nc.semaphore("at_zeroed"))
        block = prep.enter_context(nc.Block())

        @block.sync
        def _(sp):
            sp.dma_start(dirs[:, :], head_dirs.rearrange("h d -> (h d)").rearrange("(o n) -> o n", o=1)
                         .broadcast_to([P, QKW])).then_inc(loaded, 16)
            sp.dma_start(scale_b[:, :], scale.rearrange("(o n) -> o n", o=1).broadcast_to([P, 1])).then_inc(loaded, 16)
            sp.dma_start(wk_sb[:, :, :], wk.rearrange("(k p) n -> p k n", p=P)).then_inc(loaded, 16)
            sp.dma_start(w_v[:, :, :], wv.rearrange("(k p) n -> p k n", p=P)).then_inc(loaded, 16)
            sp.dma_start(w_o[:, :, :], wo.rearrange("(k p) n -> p k n", p=P)).then_inc(loaded, 16)
            sp.wait_ge(qk_cleared, 1)
            sp.dma_start(w_qk[:, :, 0:QKW], wq.rearrange("(k p) n -> p k n", p=P)).then_inc(loaded, 16)
            sp.wait_ge(zeros_done, 1)
            for b in range(B):
                sp.dma_start(q_dram[b, :, ROW_MAX:ROW_MAX + 2, :], zeros[0:H, :, :]).then_inc(zeroed, 16)
            sp.wait_ge(zeroed, B * 16)
            sp.wait_ge(loaded, 6 * 16)

        @block.vector
        def _(dve):
            nc.vector.memset(w_qk[:], 0.0).then_inc(qk_cleared, 1)
            nc.vector.memset(zeros[:], 0.0).then_inc(zeros_done, 1)
            nc.vector.memset(neg_max[:], 0.0)
            nc.vector.memset(q_rows[:].bitcast(F32), 0.0)
            dve.wait_ge(loaded, 6 * 16)
            dirs_b = dirs[:, :].rearrange("p (o n) -> p o n", o=1).broadcast_to([P, KC, QKW])
            nc.vector.tensor_tensor(on_dir[:], wk_sb[:], dirs_b, ALU.mult).then_inc(fold, 1)
            dve.wait_ge(fold, 1)
            nc.vector.tensor_reduce(on_dir_sum[:], on_dir[:].rearrange("p k (h d) -> p k h d", d=HD3),
                                    AX_X, ALU.add).then_inc(fold, 1)
            dve.wait_ge(fold, 2)
            for d in range(HD3):
                last = nc.vector.tensor_tensor(
                    along[:].rearrange("p k (h d) -> p k h d", d=HD3)[:, :, :, d], on_dir_sum[:],
                    dirs_b.rearrange("p k (h d) -> p k h d", d=HD3)[:, :, :, d], ALU.mult)
            last.then_inc(fold, 1)
            dve.wait_ge(fold, 3)
            nc.vector.scalar_tensor_tensor(out=w_qk[:, :, K0:K0 + QKW], in0=wk_sb[:], scalar=scale_b[:, 0:1],
                                           in1=along[:], op0=ALU.mult, op1=ALU.add).then_inc(fold, 1)
            nc.vector.tensor_copy(ident_bf[:], g_.ident[:]).then_inc(fold, 1)

        @block.gpsimd
        def _(pool):
            nc.gpsimd.memset(future[:], 0.0).then_inc(future_cleared, 1)
            nc.gpsimd.memset(past[:], 0.0).then_inc(future_cleared, 1)
            nc.gpsimd.memset(k_rows[:].bitcast(F32), 1.0)
            nc.gpsimd.memset(v_aug[:], 1.0)
            pool.wait_ge(future_cleared, 2)
            nc.gpsimd.affine_select(out=future[:], in_=future[:], compare_op=ALU.is_ge, fill=MASKED,
                                    base=0, pattern=[[-1, P]], channel_multiplier=1)
            nc.gpsimd.affine_select(out=past[:], in_=past[:], compare_op=ALU.is_ge, fill=MASKED,
                                    base=0, pattern=[[1, P]], channel_multiplier=-1)

    probs = sb("probs", [P, 3, HPG, CHUNK], F32)
    qk_hi = sb("qk_hi", [P, SEQ], F32R)
    qk_lo = sb("qk_lo", [P, SEQ], F32R)
    xn = sb("xn", [P, TPC, C], F32)
    xn_t = sb("xn_t", [P, KC, CHUNK], F32)
    max_t = sb("max_t", [P, NTC, CHUNK], F32)
    v_sb = sb("v_sb", [P, NT, C], F32)
    o_t = sb("o_t", [P, NG, SEQ], F32)
    o_n = xn[:, 0:2, :]
    o_n_t = xn_t[:, :, 0:2 * P]
    maxima = sb("maxima", [P, NT, HPG], F32)
    inv_sum = sb("inv_sum", [P, 2, H], F32)
    stats = sb("stats", [P, TPC, 6], F32)
    mv = sb("mv", [P, TPC, 2], F32)
    var_eps = sb("var_eps", [P, TPC], F32)
    rstd = sb("rstd", [P, TPC], F32)
    pairs = ctx.enter_context(nc.psum_tensor("at_pairs", [P, 2, 2, CHUNK], F32))
    s_t = ctx.enter_context(nc.psum_tensor("at_s_t", [P, 3, CHUNK], F32))
    o_ps = ctx.enter_context(nc.psum_tensor("at_o_ps", [P, CHUNK], F32))

    stats_done, mv_done, vareps_done, rstd_done, xn_done = (
        sem(n) for n in ("stats_done", "mv_done", "vareps_done", "rstd_done", "xn_done"))
    xt_ready, xt_copied = sem("xt_ready"), sem("xt_copied")
    qk_ready, qk_hi_done, qk_lo_done = sem("qk_ready"), sem("qk_hi_done"), sem("qk_lo_done")
    v_ready, v_copied, v_placed = sem("v_ready"), sem("v_copied"), sem("v_placed")
    saved = sem("saved")
    k_loaded = [sem(f"k_loaded{g}") for g in range(NG)]
    q_loaded = [[sem(f"q_loaded{parity}_{c}") for c in range(NTC)] for parity in range(2)]
    maxima_loaded = [sem(f"maxima_loaded{c}") for c in range(NTC)]
    scores_ready, max_done = sem("scores_ready"), sem("max_done")
    neg_hi_done, neg_max_done = sem("neg_hi_done"), sem("neg_max_done")
    mt_ready, max_t_done = sem("mt_ready"), sem("max_t_done")
    st_ready, exp_done, pv_done, o_done = (
        sem(n) for n in ("st_ready", "exp_done", "pv_done", "o_done"))
    ot_ready, inv_done, on_done = sem("ot_ready"), sem("inv_done"), sem("on_done")
    ont_ready, ont_copied = sem("ont_ready"), sem("ont_copied")
    wo_ready, x_done = sem("wo_ready"), sem("x_done")
    SAVES = 2 * len(PARTS) * HD3 * 16
    LOADS = HPG * 16

    def freed(e):
        kind, db = e[0], e[1]
        if kind == "max":
            return max_done, NG * NM, db * NG * NM + e[2] * NM + e[3] + 1
        if kind == "MT":
            return max_t_done, NG * NTC, db * NG * NTC + e[2] * NTC + e[3] + 1
        s, n = {"XT": (xt_copied, 2), "QK": (qk_lo_done, NTC), "V": (v_copied, 2), "OT": (on_done, 4),
                "AT": (ont_copied, 4), "WO": (x_done, 4)}[kind]
        return s, n, db * n + e[2] + 1

    block = ctx.enter_context(nc.Block())

    def run(eng, kinds, emit):
        def section(n, b, at):
            for e, slot, held_by in sections[n]:
                if e[0] in kinds:
                    emit(e, slot, held_by, b, at)

        section(0, -1, lambda per, c: c - per)
        section(1, 0, lambda per, c: c)
        with eng.Fori(1, B - 1) as b:
            bases = {}

            def at(per, c):
                if per not in bases:
                    bases[per] = eng.snap(b * per)
                return bases[per] + c

            section(2, b, at)
        section(3, B - 1, lambda per, c: (B - 1) * per + c)

    pool_waits, dve_waits, sp_waits = sem("pool_waits"), sem("dve_waits"), sem("sp_waits")

    def wait(eng, semaphore, value, passed=None):
        if not (isinstance(value, int) and value <= 0):
            w = eng.wait_ge(semaphore, value)
            if passed is not None:
                w.then_inc(passed, 1)

    def tokens_made(per, db, at):
        n = at(per, (db + 2) * per)
        return min(n, B * per) if isinstance(n, int) else n

    def j_bank(u, j):
        return (u * HPG + j) % 3

    GE, GM = NG * NE, NG * NM

    @block.sync
    def _(sp):
        def emit(e, slot, held_by, b, at):
            kind, db = e[0], e[1]
            if kind == "SAVE":
                wait(sp, qk_lo_done, at(NTC, (db + 1) * NTC), sp_waits)
                for n, (a, b_) in enumerate(PARTS):
                    for dram, part, p0 in ((q_dram, a, 0), (k_dram, b_, K0)):
                        for d in range(HD3):
                            sp.dma_start(dram[bass.ds(b + db, 1), :, n * HD3 + d, :].rearrange("o h t -> (o h) t"),
                                         (qk_hi, qk_lo)[part][p0 + d:p0 + QKW:HD3, :].bitcast(F32)
                                         ).then_inc(saved, 16)
            elif kind == "LK":
                g = e[2]
                wait(sp, saved, at(SAVES, (db + 1) * SAVES), sp_waits)
                wait(sp, st_ready, at(GE * HPG, ((db - 1) * NG + g + 1) * NE * HPG), sp_waits)
                for j in range(HPG):
                    sp.dma_start(k_rows[ROWS * j:ROWS * j + ROW_MAX, g, :].bitcast(F32),
                                 k_dram[bass.ds(b + db, 1), g * HPG + j, :, :].rearrange("o r t -> (o r) t")
                                 ).then_inc(k_loaded[g], 16)
            elif kind == "LQ":
                _, _, g, c = e
                s = slice(c * CHUNK, (c + 1) * CHUNK)
                wait(sp, saved, at(SAVES, (db + 1) * SAVES), sp_waits)
                used = (db * NG + g - 2) * NE + (TPC if c == 0 else NE)
                wait(sp, st_ready, at(GE * HPG, used * HPG), sp_waits)
                for j in range(HPG):
                    sp.dma_start(q_rows[ROWS * j:ROWS * j + ROW_MAX + 2, g % 2, j, s].bitcast(F32),
                                 q_dram[bass.ds(b + db, 1), g * HPG + j, :, s].rearrange("o r t -> (o r) t")
                                 ).then_inc(q_loaded[g % 2][c], 16)
            else:
                _, _, g, c = e
                wait(sp, max_t_done, at(NG * NTC, (db * NG + g) * NTC + c + 1), sp_waits)
                for j in range(HPG):
                    r = slice(ROWS * j + ROW_MAX, ROWS * j + ROW_MAX + 2)
                    sp.dma_start(q_rows[r, g % 2, j, c * CHUNK:(c + 1) * CHUNK].bitcast(F32),
                                 max_t[r, c, :]).then_inc(maxima_loaded[c], 16)

        run(sp, ("SAVE", "LK", "LQ", "NM"), emit)

    @block.gpsimd
    def _(pool):
        def emit(e, slot, held_by, b, at):
            kind, db = e[0], e[1]
            if kind == "AGGR":
                n = db * 2 + e[2]
                wait(pool, mv_done, at(2, n + 1))
                nc.gpsimd.tensor_tensor(var_eps[:, :], mv[:, :, 1], g_.eps[:, 0:TPC],
                                        ALU.add).then_inc(vareps_done, 1)
                wait(pool, vareps_done, at(2, n + 1))
                nc.gpsimd.tensor_tensor(rstd[:, :], var_eps[:, :], g_.neg_half[:, 0:TPC],
                                        ALU.pow).then_inc(rstd_done, 1)
            elif kind == "VA":
                g = e[2]
                wait(pool, v_copied, at(2, (db + 1) * 2))
                wait(pool, pv_done, at(GE, ((db - 1) * NG + g + 1) * NE), pool_waits)
                hs = slice(g * HPG, (g + 1) * HPG)
                nc.gpsimd.tensor_copy(
                    v_aug[:, :, hs, 0:HD],
                    v_sb[:, :, g * HPG * HD:(g + 1) * HPG * HD].rearrange("p i (h d) -> p i h d", d=HD),
                ).then_inc(v_placed, 1)

        run(pool, ("AGGR", "VA"), emit)

    @block.scalar
    def _(act):
        def emit(e, slot, held_by, b, at):
            kind, db = e[0], e[1]
            if kind == "S":
                _, _, g, u, j = e
                tc, k, off, n = exp_units[u]
                if j == 0:
                    wait(act, pv_done, at(GE, (db * NG + g) * NE + u - 2))
                at_n = ((db * NG + g) * NE + u) * HPG + j
                wait(act, st_ready, at(GE * HPG, at_n + 1))
                nc.scalar.activation(probs[:, u % 3, j, 0:n], s_t[:, j_bank(u, j), 0:n],
                                     ACT.Exp).then_inc(exp_done, 1)
            elif kind == "O":
                _, _, g, tc = e
                wait(act, pv_done, at(GE, (db * NG + g) * NE + (TPC if tc == 0 else NE)))
                wait(act, ot_ready, at(4, (db - 1) * 4 + 2 * tc + 2))
                nc.scalar.copy(o_t[:, g, tc * CHUNK:(tc + 1) * CHUNK], o_ps[:, :]).then_inc(o_done, 1)
            elif kind == "XT":
                h = e[2]
                wait(act, xt_ready, at(2, db * 2 + h + 1))
                wait(act, v_ready, at(2, db * 2 + h))
                wait(act, qk_ready, at(NTC, db * NTC + h))
                wait(act, wo_ready, at(4, (db - 1) * 4))
                nc.scalar.copy(xn_t[:, :, :], pairs[:, slot, :, :]).then_inc(xt_copied, 1)
            elif kind == "QK":
                tc = e[2]
                wait(act, qk_ready, at(NTC, db * NTC + tc + 1))
                wait(act, saved, at(SAVES, db * SAVES))
                nc.scalar.copy(qk_hi[:, tc * CHUNK:(tc + 1) * CHUNK], pairs[:, slot, 0, :]).then_inc(qk_hi_done, 1)
            elif kind == "V":
                h = e[2]
                wait(act, v_ready, at(2, db * 2 + h + 1))
                wait(act, v_placed, at(NG, db * NG))
                nc.scalar.copy(v_sb[:, h * TPC:(h + 1) * TPC, :],
                               pairs[:, slot, :, :].rearrange("p a (b c) -> p (a b) c", c=C)).then_inc(v_copied, 1)
            else:
                q = e[2]
                wait(act, ont_ready, at(4, db * 4 + q + 1))
                wait(act, wo_ready, at(4, db * 4 + q))
                wait(act, v_ready, tokens_made(2, db, at))
                wait(act, qk_ready, tokens_made(NTC, db, at))
                nc.scalar.copy(o_n_t,
                               pairs[:, slot, 0, :].rearrange("p (k t) -> p k t", k=KC)).then_inc(ont_copied, 1)

        run(act, ("S", "O", "XT", "QK", "V", "AT"), emit)

    @block.vector
    def _(dve):
        def token_tile(b, db, i):
            return x[:, bass.ds((b + db) * NT + i, 1), :].rearrange("p a c -> p (a c)")

        def emit(e, slot, held_by, b, at):
            kind, db = e[0], e[1]
            if kind == "STAT":
                h = e[2]
                for i in range(TPC):
                    last = nc.vector.bn_stats(stats[:, i, :], token_tile(b, db, h * TPC + i))
                last.then_inc(stats_done, 1)
            elif kind == "AGGR":
                n = db * 2 + e[2]
                wait(dve, xn_done, at(2, n))
                wait(dve, stats_done, at(2, n + 1), dve_waits)
                for i in range(TPC):
                    last = nc.vector.bn_aggr(mv[:, i, :], stats[:, i, :])
                last.then_inc(mv_done, 1)
            elif kind == "NORM":
                h = e[2]
                n = db * 2 + h
                wait(dve, rstd_done, at(2, n + 1))
                wait(dve, xt_ready, at(2, n))
                wait(dve, ont_ready, at(4, (db - 1) * 4))
                for i in range(TPC):
                    last = nc.vector.tensor_scalar(xn[:, i, :], token_tile(b, db, h * TPC + i), mv[:, i, 0:1],
                                                   rstd[:, i:i + 1], ALU.subtract, ALU.mult)
                last.then_inc(xn_done, 1)
            elif kind == "QK":
                tc = e[2]
                wait(dve, qk_hi_done, at(NTC, db * NTC + tc + 1))
                wait(dve, saved, at(SAVES, db * SAVES))
                s = slice(tc * CHUNK, (tc + 1) * CHUNK)
                nc.vector.tensor_tensor(qk_lo[:, s], pairs[:, slot, 0, :], qk_hi[:, s],
                                        ALU.subtract).then_inc(qk_lo_done, 1)
            elif kind == "max":
                _, _, g, m = e
                i, js = max_units[m]
                n = (i + 1) * P
                wait(dve, scores_ready, at(GM, (db * NG + g) * NM + m + 1))
                if m in (0, first_half):
                    wait(dve, neg_max_done, at(NG * NTC, (db * NG + g) * NTC - 1 + (m > 0)))
                if len(js) == 2:
                    nc.vector.tensor_reduce(maxima[:, i, js[0]:js[0] + 2], pairs[:, slot, :, 0:n], AX_X,
                                            ALU.max).then_inc(max_done, 1)
                else:
                    nc.vector.tensor_reduce(maxima[:, i, js[0]:js[0] + 1],
                                            pairs[:, slot, :, :].rearrange("p a n -> p (a n)")[:, 0:n], AX_X,
                                            ALU.max).then_inc(max_done, 1)
            elif kind == "MM":
                _, _, g, c = e
                n = (db * NG + g) * NTC + c
                rows = neg_max[:, :, :].rearrange("p i (j r) -> p i j r", r=ROWS)
                m = maxima[:, c * TPC:(c + 1) * TPC, :]
                wait(dve, max_done, at(GM, (db * NG + g) * NM + (first_half if c == 0 else NM)))
                wait(dve, mt_ready, at(NG * NTC, n))
                nc.vector.tensor_scalar(rows[:, :, :, ROW_MAX].bitcast(F32R), m, -1.0, None,
                                        ALU.mult).then_inc(neg_hi_done, 1)
                wait(dve, neg_hi_done, at(NG * NTC, n + 1))
                nc.vector.scalar_tensor_tensor(out=rows[:, :, :, ROW_MAX + 1].bitcast(F32R), in0=m, scalar=-1.0,
                                               in1=rows[:, :, :, ROW_MAX], op0=ALU.mult,
                                               op1=ALU.subtract).then_inc(neg_max_done, 1)
            elif kind == "MT":
                _, _, g, c = e
                n = (db * NG + g) * NTC + c
                wait(dve, mt_ready, at(NG * NTC, n + 1))
                wait(dve, maxima_loaded[c], at(NG * LOADS, (db * NG + g) * LOADS))
                nc.vector.tensor_copy(max_t[:, c, :], pairs[:, slot, 0, :]).then_inc(max_t_done, 1)
            elif kind == "OT":
                q = e[2]
                n = db * 4 + q
                heads = pairs[:, slot, :, :].rearrange("p a (h r) -> p a h r", r=2 * HD)
                wait(dve, ot_ready, at(4, n + 1))
                wait(dve, on_done, at(4, n))
                nc.vector.reciprocal(inv_sum[:, :, :], heads[:, :, :, HD]).then_inc(inv_done, 1)
                wait(dve, inv_done, at(4, n + 1))
                wait(dve, ont_ready, at(4, n))
                wait(dve, xt_ready, tokens_made(2, db, at))
                nc.vector.tensor_tensor(
                    o_n.rearrange("p a (h d) -> p a h d", d=HD), heads[:, :, :, 0:HD],
                    inv_sum[:, :, :].rearrange("p a (h o) -> p a h o", o=1).broadcast_to([P, 2, H, HD]),
                    ALU.mult).then_inc(on_done, 1)
            else:
                q = e[2]
                wait(dve, wo_ready, at(4, db * 4 + q + 1))
                two = x[:, bass.ds((b + db) * NT + 2 * q, 2), :]
                nc.vector.tensor_tensor(two, pairs[:, slot, 0, :].rearrange("p (a c) -> p a c", c=C), two,
                                        ALU.add).then_inc(x_done, 1)

        run(dve, ("STAT", "AGGR", "NORM", "QK", "max", "MM", "MT", "OT", "WO"), emit)

    @block.tensor
    def _(pe):
        def emit(e, slot, held_by, b, at):
            kind, db = e[0], e[1]
            if held_by is not None:
                semaphore, per, count = freed(held_by)
                wait(pe, semaphore, at(per, count))
            if kind == "S":
                _, _, g, u, j = e
                tc, k, off, n = exp_units[u]
                if j == 0 and u in (0, TPC):
                    wait(pe, maxima_loaded[tc], at(NG * LOADS, (db * NG + g + 1) * LOADS))
                wait(pe, exp_done, at(GE * HPG, ((db * NG + g) * NE + u) * HPG + j - 2))
                diagonal = k >= tc * TPC
                last = nc.tensor.matmul(s_t[:, j_bank(u, j), 0:n], k_rows[:, g, k * P:(k + 1) * P],
                                        q_rows[:, g % 2, j, tc * CHUNK + off:(tc + 1) * CHUNK],
                                        start=True, stop=not diagonal)
                if diagonal:
                    last = nc.tensor.matmul(s_t[:, j_bank(u, j), 0:P], ident_bf[:, :], past[:, :],
                                            start=False, stop=True)
                last.then_inc(st_ready, 1)
            elif kind == "PV":
                _, _, g, u = e
                tc, k, off, n = exp_units[u]
                if u == 0:
                    wait(pe, v_placed, at(NG, db * NG + g + 1))
                if k == 0:
                    wait(pe, o_done, at(NG * 2, (db * NG + g) * 2 + tc))
                wait(pe, exp_done, at(GE * HPG, ((db * NG + g) * NE + u + 1) * HPG))
                for j in range(HPG):
                    last = nc.tensor.matmul(o_ps[ROWS * j:ROWS * (j + 1), off:off + n],
                                            v_aug[:, k, g * HPG + j, :], probs[:, u % 3, j, 0:n],
                                            start=(k == 0), stop=(k == (tc + 1) * TPC - 1))
                last.then_inc(pv_done, 1)
            elif kind == "max":
                _, _, g, m = e
                i, js = max_units[m]
                n = (i + 1) * P
                if m == 0:
                    wait(pe, k_loaded[g], at(LOADS, (db + 1) * LOADS))
                if m in (0, first_half):
                    c = int(m > 0)
                    wait(pe, q_loaded[g % 2][c], at(NG // 2 * LOADS, (db * (NG // 2) + g // 2 + 1) * LOADS))
                for a, j in enumerate(js):
                    for c0 in range(0, n, CHUNK):
                        c1 = min(n, c0 + CHUNK)
                        nc.tensor.matmul(pairs[:, slot, a + c0 // CHUNK, 0:c1 - c0],
                                         q_rows[:, g % 2, j, i * P:(i + 1) * P], k_rows[:, g, c0:c1],
                                         start=True, stop=(c1 < n))
                for a, j in enumerate(js):
                    bank, end = a + (n - 1) // CHUNK, (n - 1) % CHUNK + 1
                    last = nc.tensor.matmul(pairs[:, slot, bank, end - P:end], ident_bf[:, :], future[:, :],
                                            start=False, stop=True)
                last.then_inc(scores_ready, 1)
            elif kind == "MT":
                _, _, g, c = e
                wait(pe, neg_max_done, at(NG * NTC, (db * NG + g) * NTC + c + 1))
                for i in range(TPC):
                    last = nc.tensor.transpose(pairs[:, slot, 0, i * P:(i + 1) * P], neg_max[:, i, :], g_.ident[:, :])
                last.then_inc(mt_ready, 1)
            elif kind == "XT":
                h = e[2]
                wait(pe, xn_done, at(2, db * 2 + h + 1))
                for kc in range(KC):
                    for i in range(TPC):
                        last = nc.tensor.transpose(pairs[:, slot, kc, i * P:(i + 1) * P],
                                                   xn[:, i, kc * P:(kc + 1) * P], g_.ident[:, :])
                last.then_inc(xt_ready, 1)
            elif kind == "QK":
                tc = e[2]
                wait(pe, xt_copied, at(2, db * 2 + tc + 1))
                for kc in range(KC):
                    last = nc.tensor.matmul(pairs[:, slot, 0, :], w_qk[:, kc, :],
                                            xn_t[:, kc, :],
                                            start=(kc == 0), stop=(kc == KC - 1))
                last.then_inc(qk_ready, 1)
            elif kind == "V":
                h = e[2]
                wait(pe, xt_copied, at(2, db * 2 + h + 1))
                for i in range(TPC):
                    t = i * P
                    for kc in range(KC):
                        last = nc.tensor.matmul(pairs[:, slot, i // 2, i % 2 * C:(i % 2 + 1) * C],
                                                xn_t[:, kc, t:t + P], w_v[:, kc, :],
                                                start=(kc == 0), stop=(kc == KC - 1))
                last.then_inc(v_ready, 1)
            elif kind == "OT":
                q = e[2]
                wait(pe, o_done, at(NG * 2, (db * NG + NG - 1) * 2 + q // 2 + 1))
                for a in range(2):
                    for g in range(NG):
                        t = (2 * q + a) * P
                        last = nc.tensor.transpose(pairs[:, slot, a, g * P:(g + 1) * P], o_t[:, g, t:t + P],
                                                   g_.ident[:, :])
                last.then_inc(ot_ready, 1)
            elif kind == "AT":
                q = e[2]
                wait(pe, on_done, at(4, db * 4 + q + 1))
                for kc in range(KC):
                    for a in range(2):
                        t = (kc * 2 + a) * P
                        last = nc.tensor.transpose(pairs[:, slot, 0, t:t + P], o_n[:, a, kc * P:(kc + 1) * P],
                                                   g_.ident[:, :])
                last.then_inc(ont_ready, 1)
            else:
                q = e[2]
                wait(pe, ont_copied, at(4, db * 4 + q + 1))
                for a in range(2):
                    for kc in range(KC):
                        last = nc.tensor.matmul(pairs[:, slot, 0, a * C:(a + 1) * C], o_n_t[:, kc, a * P:(a + 1) * P],
                                                w_o[:, kc, :], start=(kc == 0), stop=(kc == KC - 1))
                last.then_inc(wo_ready, 1)

        run(pe, ("S", "PV", "max", "MT", "XT", "QK", "V", "OT", "AT", "WO"), emit)


def macaron(nc, x_in, wq, wk, wv, wo, head_dirs, scale, w_gate, w_up, w_down, out):
    B, SEQ, C = x_in.shape
    T = B * SEQ // P
    x_tiles = x_in.rearrange("b (i p) c -> p (b i) c", p=P)
    out_tiles = out.rearrange("b (i p) c -> p (b i) c", p=P)
    with ExitStack() as ctx:
        g = Buffers()
        g.x = ctx.enter_context(nc.sbuf_tensor("x", [P, T, C], F32))
        g.ident = ctx.enter_context(nc.sbuf_tensor("ident", [P, P], F32))
        g.ones = ctx.enter_context(nc.sbuf_tensor("ones", [P, 1], F32))
        g.neg_half = ctx.enter_context(nc.sbuf_tensor("neg_half", [P, 8], F32))
        g.eps = ctx.enter_context(nc.sbuf_tensor("eps", [P, 8], F32))
        g.consts_done = ctx.enter_context(nc.semaphore("consts_done"))
        g.N_CONSTS = 5
        with ExitStack() as consts:
            block = consts.enter_context(nc.Block())

            @block.gpsimd
            def _(pool):
                nc.gpsimd.memset(g.ones[:], 1.0).then_inc(g.consts_done, 1)
                nc.gpsimd.memset(g.neg_half[:], -0.5).then_inc(g.consts_done, 1)
                nc.gpsimd.memset(g.ident[:], 0.0).then_inc(g.consts_done, 1)
                nc.gpsimd.memset(g.eps[:], EPS).then_inc(g.consts_done, 1)
                pool.wait_ge(g.consts_done, 4)
                nc.gpsimd.affine_select(out=g.ident[:], in_=g.ident[:], compare_op=ALU.not_equal, fill=1.0,
                                        base=0, pattern=[[-1, P]], channel_multiplier=1).then_inc(g.consts_done, 1)
        with ExitStack() as stage:
            ffn_stage(nc, stage, g, "ffn1", w_gate, w_up, w_down, x_tiles, None)
        with ExitStack() as stage:
            attention_stage(nc, stage, g, wq, wk, wv, wo, head_dirs, scale, B)
        with ExitStack() as stage:
            ffn_stage(nc, stage, g, "ffn2", w_gate, w_up, w_down, None, out_tiles)


def kernel(L0_attn_x, L0_attn_wq, L0_attn_wk, L0_attn_wv, L0_attn_wo, L0_attn_head_dirs, L0_attn_scale,
           L0_ffn_w_gate, L0_ffn_w_up, L0_ffn_w_down):
    import numpy as np
    import concourse.bacc as bacc
    from concourse.bass_utils import run_bass_kernel_spmd

    arrays = {
        "x_in": L0_attn_x, "wq": L0_attn_wq, "wk": L0_attn_wk, "wv": L0_attn_wv, "wo": L0_attn_wo,
        "head_dirs": L0_attn_head_dirs, "scale": L0_attn_scale,
        "w_gate": np.asarray(L0_ffn_w_gate).T, "w_up": np.asarray(L0_ffn_w_up).T,
        "w_down": np.asarray(L0_ffn_w_down).T,
    }
    arrays = {name: np.ascontiguousarray(a) for name, a in arrays.items()}
    nc = bacc.Bacc("TRN2", target_bir_lowering=False, num_devices=1)
    aps = [nc.dram_tensor(name, a.shape, mybir.dt.from_np(a.dtype), kind="ExternalInput").ap()
           for name, a in arrays.items()]
    out = nc.dram_tensor("out", arrays["x_in"].shape, F32, kind="ExternalOutput").ap()
    macaron(nc, *aps, out)
    result = run_bass_kernel_spmd(nc, [arrays], core_ids=[0])
    return result.results[0]["out"]
```

```python
from contextlib import ExitStack

import concourse.bass as bass
from concourse import mybir

F32 = mybir.dt.float32
F32R = mybir.dt.float32r
BF16 = mybir.dt.bfloat16
I32 = mybir.dt.int32
ALU = mybir.AluOpType
ACT = mybir.ActivationFunctionType
AX_X = mybir.AxisListType.X

P = 128
CHUNK = 512
TPC = CHUNK // P
EPS = 1e-5
W_SCALE = 1.0 / 127.0
EXACT_MAX = 2048.0
MASKED = -1.0e30


class Buffers:
    pass


def ffn_stage(nc, ctx, g, tag, w_gate, w_up, w_down, x_in, x_out, find_flag):
    C = w_gate.shape[0]
    HID = w_gate.shape[1]
    KC = C // P
    MH = HID // P
    T = g.x.shape[1]
    NCH = T // TPC
    TANH_SCALE = 0.5 * W_SCALE
    OUT_SCALE = 0.5 * 0.5 * W_SCALE * W_SCALE * W_SCALE
    x = g.x

    def sb(name, shape, dt):
        return ctx.enter_context(nc.sbuf_tensor(f"{tag}_{name}", shape, dt))

    def sem(name):
        return ctx.enter_context(nc.semaphore(f"{tag}_{name}"))

    w_hi = sb("w_hi", [P, 3 * KC * HID], F32R)
    w_lo = sb("w_lo", [P, 3 * KC * HID], F32R)
    NW = KC * HID

    def view(w, n):
        k = KC if n < 2 else MH
        return w[:, n * NW:(n + 1) * NW].rearrange("p (k n) -> p k n", k=k)

    parts = [slice(n * NW, (n + 1) * NW) for n in range(3)]
    w_f32 = sb("w_f32", [P, 3 * NW], F32)
    w_int = w_f32[:, :].bitcast(I32)
    int_loaded = [sem(f"int_loaded{n}") for n in range(3)]
    hi_done = sem("hi_done")
    f32_done = sem("f32_done")
    lo_done = sem("lo_done")
    if find_flag:
        int_max = sb("int_max", [P, 3], F32)
        above = sb("above", [P, 3], F32)
        max_done, above_done, sum_done = sem("max_done"), sem("above_done"), sem("sum_done")

    xn = sb("xn", [P, 2, TPC, C], F32)
    x_hi = sb("x_hi", [P, 2, KC, CHUNK], F32R)
    x_lo = sb("x_lo", [P, 2, KC, CHUNK], F32R)
    h_hi = sb("h_hi", [P, 2, MH, CHUNK], F32R)
    h_lo = sb("h_lo", [P, 2, MH, CHUNK], F32R)
    tanh_sb = sb("tanh_sb", [P, 2, CHUNK], F32)
    act_sb = sb("act_sb", [P, 2, CHUNK], F32)
    h_sb = sb("h_sb", [P, 3, CHUNK], F32)
    stats = sb("stats", [P, TPC, 6], F32)
    mv = sb("mv", [P, TPC, 2], F32)
    var_eps = sb("var_eps", [P, TPC], F32)
    rstd = sb("rstd", [P, TPC], F32)
    gate_up = ctx.enter_context(nc.psum_tensor(f"{tag}_gate_up", [P, 2, 2, CHUNK], F32))
    xt_ps = ctx.enter_context(nc.psum_tensor(f"{tag}_xt_ps", [P, KC, CHUNK], F32))
    y_ps = ctx.enter_context(nc.psum_tensor(f"{tag}_y_ps", [P, TPC // 2, 2, C], F32))

    x_loaded = [sem(f"x_loaded{p}") for p in range(2)]
    stats_done = sem("stats_done")
    mv_done = sem("mv_done")
    vareps_done = sem("vareps_done")
    rstd_done = sem("rstd_done")
    xn_done = sem("xn_done")
    xt_done = sem("xt_done")
    xhi_done = sem("xhi_done")
    xlo_done = sem("xlo_done")
    gate_done = sem("gate_done")
    up_done = sem("up_done")
    tanh_done = sem("tanh_done")
    act_done = sem("act_done")
    h_done = sem("h_done")
    hhi_done = sem("hhi_done")
    hlo_done = sem("hlo_done")
    y_done = sem("y_done")
    x_done = sem("x_done")
    x_stored = [sem(f"x_stored{p}") for p in range(2)]

    def chunks(eng, step, started=False):
        if not started:
            step(0, 0, True, False)
        step(1, 1, False, False)
        with eng.Fori(1, NCH // 2 - 1) as k:
            c2 = eng.snap(k * 2)
            step(c2, 0, False, False)
            step(c2 + 1, 1, False, False)
        step(NCH - 2, 0, False, False)
        step(NCH - 1, 1, False, True)

    block = ctx.enter_context(nc.Block())

    def tiles(c):
        return x[:, bass.ds(c * TPC, TPC), :]

    def half(c, n):
        return x[:, bass.ds(c * TPC + 2 * n, 2), :]

    @block.sync
    def _(sp):
        def load(c, p, first, last):
            if not first and not (isinstance(c, int) and c == 1):
                sp.wait_ge(x_loaded[p], (c - p) * 8)
            sp.dma_start(tiles(c), x_in[:, bass.ds(c * TPC, TPC), :]).then_inc(x_loaded[p], 16)

        def store(c, p, first, last):
            sp.wait_ge(x_done, (c + 1) * 2)
            sp.dma_start(x_out[:, bass.ds(c * TPC, TPC), :], tiles(c)).then_inc(x_stored[p], 16)

        def load_weight(n):
            w = (w_gate, w_up, w_down)[n]
            sp.dma_start(w_int[:, parts[n]].rearrange("p (k n) -> p k n", k=w.shape[0] // P),
                         w.rearrange("(k p) n -> p k n", p=P)).then_inc(int_loaded[n], 16)

        def load_and_weights(c, p, first, last):
            load(c, p, first, last)
            if first:
                for n in range(3):
                    load_weight(n)

        if x_in is not None:
            chunks(sp, load_and_weights)
        else:
            for n in range(3):
                load_weight(n)
        if x_out is not None:
            chunks(sp, store)
            for p in range(2):
                sp.wait_ge(x_stored[p], NCH // 2 * 16)

    @block.gpsimd
    def _(pool):
        def rstd_of(c):
            pool.wait_ge(mv_done, c + 1)
            nc.gpsimd.tensor_tensor(var_eps[:, :], mv[:, :, 1], g.eps[:, 0:TPC], ALU.add).then_inc(vareps_done, 1)
            pool.wait_ge(vareps_done, c + 1)
            nc.gpsimd.tensor_tensor(rstd[:, :], var_eps[:, :], g.neg_half[:, 0:TPC],
                                    ALU.pow).then_inc(rstd_done, 1)

        def step(c, p, first, last):
            if not last:
                rstd_of(c + 1)
            for m in range(MH):
                n = c * MH + m
                pool.wait_ge(h_done, n + 1)
                pool.wait_ge(hhi_done, n + 1)
                if not first and not (isinstance(c, int) and c == 1):
                    pool.wait_ge(y_done, (c - 1) * 2)
                nc.gpsimd.tensor_tensor(h_lo[:, p, m, :], h_sb[:, m % 3, :], h_hi[:, p, m, :],
                                        ALU.subtract).then_inc(hlo_done, 1)

        pool.wait_ge(g.consts_done, g.N_CONSTS)
        rstd_of(0)
        pool.wait_ge(g.flag_done, 1)
        has_low = pool.value_load(g.flag[0:1, 0:1], min_val=0, max_val=1 << 30)
        with pool.If(has_low > 0):
            for n in range(3):
                pool.wait_ge(hi_done, n + 1)
                nc.gpsimd.tensor_tensor(w_lo[:, parts[n]], w_f32[:, parts[n]], w_hi[:, parts[n]],
                                        ALU.subtract).then_inc(lo_done, 1)
        chunks(pool, step)

    @block.scalar
    def _(act):
        def split_x(c, p):
            for kc in range(KC):
                act.wait_ge(xt_done, c * KC + kc + 1)
                nc.scalar.copy(x_hi[:, p, kc, :], xt_ps[:, kc, :]).then_inc(xhi_done, 1)

        def step(c, p, first, last):
            def h_high(m):
                n = c * MH + m
                act.wait_ge(h_done, n + 1)
                if not first and not (isinstance(c, int) and c == 1):
                    act.wait_ge(y_done, (c - 1) * 2)
                nc.scalar.copy(h_hi[:, p, m, :], h_sb[:, m % 3, :]).then_inc(hhi_done, 1)

            for m in range(MH):
                n = c * MH + m
                act.wait_ge(gate_done, n + 1)
                if not (first and m < 2):
                    act.wait_ge(act_done, n - 1)
                nc.scalar.activation(tanh_sb[:, m % 2, :], gate_up[:, m % 2, 0, :], ACT.Tanh,
                                     scale=TANH_SCALE).then_inc(tanh_done, 1)
                if m >= 1:
                    h_high(m - 1)
                if m == 4 and not last:
                    split_x(c + 1, 1 - p)
            h_high(MH - 1)

        def f32_weight(n):
            act.wait_ge(int_loaded[n], 16)
            nc.scalar.copy(w_f32[:, parts[n]], w_int[:, parts[n]]).then_inc(f32_done, 1)

        def high_weight(n):
            act.wait_ge(f32_done, n + 1)
            nc.scalar.copy(w_hi[:, parts[n]], w_f32[:, parts[n]]).then_inc(hi_done, 1)

        f32_weight(0)
        high_weight(0)
        f32_weights = (1, 2) if find_flag else ()
        for n in f32_weights:
            f32_weight(n)
        split_x(0, 0)
        for n in (1, 2):
            if n not in f32_weights:
                f32_weight(n)
            high_weight(n)
        chunks(act, step)

    @block.vector
    def _(dve):
        def ln_stats(c, p):
            if x_in is not None:
                dve.wait_ge(x_loaded[p], (c - p) * 8 + 16)
            for i in range(TPC):
                last = nc.vector.bn_stats(stats[:, i, :], x[:, bass.ds(c * TPC + i, 1), :].rearrange("p a c -> p (a c)"))
            last.then_inc(stats_done, 1)

        def ln_gather():
            for i in range(TPC):
                last = nc.vector.bn_aggr(mv[:, i, :], stats[:, i, :])
            last.then_inc(mv_done, 1)

        def ln_norm(c, p):
            dve.wait_ge(rstd_done, c + 1)
            if not (isinstance(c, int) and c < 2):
                dve.wait_ge(xt_done, (c - 1) * KC)
            for i in range(TPC):
                last = nc.vector.tensor_scalar(xn[:, p, i, :], x[:, bass.ds(c * TPC + i, 1), :].rearrange("p a c -> p (a c)"),
                                               mv[:, i, 0:1], rstd[:, i:i + 1], ALU.subtract, ALU.mult)
            last.then_inc(xn_done, 1)

        def split_x(c, p):
            for kc in range(KC):
                dve.wait_ge(xhi_done, c * KC + kc + 1)
                nc.vector.tensor_tensor(x_lo[:, p, kc, :], xt_ps[:, kc, :], x_hi[:, p, kc, :],
                                        ALU.subtract).then_inc(xlo_done, 1)

        def residual(c, n):
            dve.wait_ge(y_done, c * 2 + n + 1)
            nc.vector.scalar_tensor_tensor(out=half(c, n), in0=y_ps[:, n, :, :], scalar=OUT_SCALE,
                                           in1=half(c, n), op0=ALU.mult, op1=ALU.add).then_inc(x_done, 1)

        def step(c, p, first, last):
            def gate(m):
                n = c * MH + m
                dve.wait_ge(tanh_done, n + 1)
                nc.vector.scalar_tensor_tensor(out=act_sb[:, m % 2, :], in0=tanh_sb[:, m % 2, :], scalar=1.0,
                                               in1=gate_up[:, m % 2, 0, :], op0=ALU.add,
                                               op1=ALU.mult).then_inc(act_done, 1)

            def up(m):
                n = c * MH + m
                dve.wait_ge(act_done, n + 1)
                dve.wait_ge(up_done, n + 1)
                if not (first and m < 3):
                    dve.wait_ge(hlo_done, n - 2)
                nc.vector.tensor_tensor(h_sb[:, m % 3, :], act_sb[:, m % 2, :], gate_up[:, m % 2, 1, :],
                                        ALU.mult).then_inc(h_done, 1)

            for m in range(MH):
                if m == 0 and not last:
                    ln_stats(c + 1, 1 - p)
                    dve.wait_ge(stats_done, c + 2)
                    dve.wait_ge(xn_done, c + 1)
                gate(m)
                if m == 0 and not last:
                    ln_gather()
                if m == 2 and not last:
                    ln_norm(c + 1, 1 - p)
                up(m)
                if m in (3, 4) and not first:
                    residual(c - 1, m - 3)
                if m == 4 and not last:
                    split_x(c + 1, 1 - p)

        ln_stats(0, 0)
        dve.wait_ge(stats_done, 1)
        ln_gather()

        def largest_integer(n):
            if find_flag:
                dve.wait_ge(f32_done, n + 1)
                nc.vector.tensor_reduce(int_max[:, n:n + 1], w_f32[:, parts[n]], AX_X, ALU.max,
                                        apply_absolute_value=True).then_inc(max_done, 1)

        ln_norm(0, 0)
        largest_integer(0)
        largest_integer(1)
        largest_integer(2)
        if find_flag:
            dve.wait_ge(max_done, 3)
            nc.vector.tensor_scalar(above[:, :], int_max[:, :], EXACT_MAX, None, ALU.is_gt).then_inc(above_done, 1)
            dve.wait_ge(sum_done, 1)
            nc.vector.tensor_reduce(g.flag[:, :], gate_up[0:1, 0, 0, 0:3], AX_X, ALU.max).then_inc(g.flag_done, 1)
        split_x(0, 0)
        chunks(dve, step)
        residual(NCH - 1, 0)
        residual(NCH - 1, 1)

    @block.tensor
    def _(pe):
        def transpose_x(c, p):
            pe.wait_ge(xn_done, c + 1)
            if not (isinstance(c, int) and c == 0):
                pe.wait_ge(xlo_done, c * KC)
            for kc in range(KC):
                for i in range(TPC):
                    last = nc.tensor.transpose(xt_ps[:, kc, i * P:(i + 1) * P],
                                               xn[:, p, i, kc * P:(kc + 1) * P], g.ident[:, :])
                last.then_inc(xt_done, 1)

        def products(w, n, m, moving_hi, moving_lo, exact):
            for kc in range(KC):
                s = slice(m * P, (m + 1) * P)
                yield view(w_hi, n)[:, kc, s], moving_hi[:, kc, :]
                yield view(w_hi, n)[:, kc, s], moving_lo[:, kc, :]
                if not exact:
                    yield view(w_lo, n)[:, kc, s], moving_hi[:, kc, :]
                    yield view(w_lo, n)[:, kc, s], moving_lo[:, kc, :]

        def stage(exact):
            def down(c, p, i):
                if i == 0:
                    pe.wait_ge(hlo_done, (c + 1) * MH)
                if i % 2 == 0 and not (isinstance(c, int) and c == 0):
                    pe.wait_ge(x_done, c * 2 - 1 + i // 2)
                ops = []
                for m in range(MH):
                    s = slice(i * P, (i + 1) * P)
                    ops.append((h_hi[:, p, m, s], view(w_hi, 2)[:, m, :]))
                    ops.append((h_lo[:, p, m, s], view(w_hi, 2)[:, m, :]))
                    if not exact:
                        ops.append((h_hi[:, p, m, s], view(w_lo, 2)[:, m, :]))
                        ops.append((h_lo[:, p, m, s], view(w_lo, 2)[:, m, :]))
                for k, (stationary, moving) in enumerate(ops):
                    last = nc.tensor.matmul(y_ps[:, i // 2, i % 2, :], stationary, moving,
                                            start=(k == 0), stop=(k == len(ops) - 1))
                if i % 2:
                    last.then_inc(y_done, 1)

            def step(c, p, first, last):
                pe.wait_ge(xlo_done, (c + 1) * KC)
                if first and not exact:
                    pe.wait_ge(lo_done, 3)
                for m in range(MH):
                    n = c * MH + m
                    if not (first and m < 2):
                        pe.wait_ge(h_done, n - 1)
                    for which, done in ((0, gate_done), (1, up_done)):
                        if first and m == 0:
                            pe.wait_ge(hi_done, which + 1)
                        ops = list(products(w_hi, which, m, x_hi[:, p], x_lo[:, p], exact))
                        for k, (stationary, moving) in enumerate(ops):
                            last_mm = nc.tensor.matmul(gate_up[:, m % 2, which, :], stationary, moving,
                                                       start=(k == 0), stop=(k == len(ops) - 1))
                        last_mm.then_inc(done, 1)
                    if m == 3 and not last:
                        transpose_x(c + 1, 1 - p)
                    if not first and m in (1, 2, 3, 4):
                        down(c - 1, 1 - p, m - 1)

            step(0, 0, True, False)
            pe.wait_ge(hi_done, 3)
            chunks(pe, step, started=True)
            for i in range(TPC):
                down(NCH - 1, 1, i)

        pe.wait_ge(g.consts_done, g.N_CONSTS)
        transpose_x(0, 0)
        if find_flag:
            pe.wait_ge(above_done, 1)
            nc.tensor.matmul(gate_up[0:1, 0, 0, 0:3], g.ones[:, 0:1], above[:, :],
                             start=True, stop=True).then_inc(sum_done, 1)
        pe.wait_ge(g.flag_done, 1)
        has_low = pe.value_load(g.flag[0:1, 0:1], min_val=0, max_val=1 << 30)
        with pe.If(has_low > 0):
            stage(exact=False)
        with pe.Else():
            stage(exact=True)
        pe.nop()


HPG = 4
ROWS = 32
HD3 = 3
PARTS = ((0, 0), (0, 1), (1, 0), (1, 1))
ROW_MAX = HD3 * len(PARTS)


def attention_plan(NT, NG):
    per = CHUNK // P
    exp_units = []
    for tc in range(NT // per):
        for k in range((tc + 1) * per):
            off = max(0, k - tc * per) * P
            exp_units.append((tc, k, off, CHUNK - off))
    exp_calls = []
    for u, (_, _, _, n) in enumerate(exp_units):
        heads = min(HPG, 1 << (CHUNK // n).bit_length() - 1)
        exp_calls += [(u, tuple(range(j, j + heads))) for j in range(0, HPG, heads)]
    max_units = []
    for i in range(NT):
        heads = HPG if (i + 1) * P <= CHUNK // 2 else 2 if (i + 1) * P <= CHUNK else 1
        max_units += [(i, tuple(range(j, j + heads))) for j in range(0, HPG, heads)]
    first_half = len([1 for i, _ in max_units if i < per])
    NE, NM = len(exp_units), len(max_units)
    ring = ("max", "MT", "XT", "QK", "V", "OT", "AT", "WO")

    def cost(e):
        kind = e[0]
        if kind == "S":
            _, k, off, n = exp_units[e[3]]
            return len(e[4]) * (0.42 * n + (54 if k * P >= exp_units[e[3]][0] * CHUNK else 0)) + 54, \
                60 + len(e[4]) * 0.84 * n, "act"
        if kind == "PV":
            return 70 + 1.67 * exp_units[e[3]][3], 0, None
        if kind == "max":
            i, js = max_units[e[3]]
            n = len(js) * (i + 1) * P
            return 0.42 * n + 60 * len(js) + 50, 80 + 1.04 * n, "dve"
        return {"MT": (220, 600, "dve"), "XT": (860, 900, "act"), "QK": (1720, 1100, "act"),
                "V": (3440, 900, "act"), "OT": (860, 1000, "dve"), "AT": (430, 480, "act"),
                "WO": (1720, 600, "dve"), "MM": (0, 400, "dve"), "O": (0, 480, "act"),
                "STAT": (0, 1340, "dve"), "AGGR": (0, 300, "dve"), "NORM": (0, 1340, "dve")}.get(kind, (0, 0, None))

    def group(n):
        return n // NG, n % NG

    def streams(s):
        e_stream = []
        for u in range(NE):
            e_stream += [("S", 0, s, u, js) for v, js in exp_calls if v == u]
            e_stream += [("PV", 0, s, u - 1)] if u else [("PV", *group(s - 1), NE - 1), ("O", *group(s - 1), 1)]
            if u == per:
                e_stream.append(("O", 0, s, 0))
        nxt = group(s + 1)
        m_stream = [("MT", 0, s, 1), ("NM", 0, s, 1)]
        m_stream += [("max", *nxt, n) for n in range(first_half)] + [("MM", *nxt, 0)]
        m_stream += [("max", *nxt, n) for n in range(first_half, NM)] + [("MM", *nxt, 1)]
        m_stream[first_half + 5:first_half + 5] = [("MT", *nxt, 0), ("NM", *nxt, 0)]
        finish = {db: [(kind, db, q) for kind in ("OT", "AT", "WO") for q in (2 if db else 0, 3 if db else 1)]
                  for db in (-1, 0)}
        x_stream = {
            0: finish[-1] + [("STAT", 1, 0), ("AGGR", 1, 0), ("NORM", 1, 0), ("XT", 1, 0), ("QK", 1, 0),
                                        ("STAT", 1, 1), ("AGGR", 1, 1)],
            1: [("NORM", 1, 1), ("V", 1, 0), ("XT", 1, 1), ("QK", 1, 1), ("SAVE", 1, 0)],
            2: [("V", 1, 1)],
            3: finish[0]}.get(s, [])
        return [e_stream, m_stream, x_stream]

    def at_unit(s, u):
        out = []
        if u == 0:
            out.append(("LQ", *group(s + 1), 1))
        if u == 5:
            out.append(("LQ", *group(s + 2), 0))
        return out + {(0, 0): [("LK", 0, NG - 1)], (0, 4): [("VA", 0, NG - 1)],
                      (2, 1): [("SAVE", 1, 1)], (2, 6): [("LK", 1, 0), ("LK", 1, 1)], (3, 2): [("LK", 1, 2)],
                      (3, 4): [("VA", 1, 0)], (3, 5): [("VA", 1, 1)], (3, 6): [("VA", 1, 2)]}.get((s, u), [])

    HOP = 400.0
    LATE = 100.0
    free = {"pe": 0.0, "act": 0.0, "dve": 0.0}
    done = {}
    banks, pairs_used, exps = [], [], []

    def ready(e):
        kind = e[0]
        t = 0.0
        if kind in ring and len(pairs_used) >= 2:
            t = pairs_used[-2] + HOP
        if kind == "S" and len(exps) >= 3:
            t = max(t, exps[-3] + HOP)
        if kind == "PV":
            t = max(t, done.get(("S", e[2], e[3]), 0.0) + HOP)
        before = {"MT": "MM", "XT": "NORM", "QK": "XT", "V": "XT", "AT": "OT", "WO": "AT", "NORM": "AGGR"}.get(kind)
        if before:
            t = max(t, done.get((before,) + tuple(e[2:]), 0.0) + HOP + (1500 if kind == "NORM" else 0))
        if kind == "OT":
            t = max(t, done.get(("O", NG - 1, e[2] // 2), 0.0) + HOP)
        return t

    def place(e):
        pe, reader, engine = cost(e)
        if pe:
            free["pe"] = max(free["pe"], ready(e)) + pe
        if engine:
            start = max(free[engine], (free["pe"] + HOP) if pe else ready(e))
            free[engine] = start + reader
            if e[0] in ring:
                pairs_used.append(free[engine])
            if e[0] == "S":
                exps.append(free[engine])
                done[("S", e[2], e[3])] = free[engine]
            else:
                done[(e[0],) + tuple(e[2:])] = free[engine]

    def stage(s):
        events = []
        queues = streams(s)
        weights = [[max(1.0, cost(e)[0]) for e in q] for q in queues]
        totals = [sum(w) or 1.0 for w in weights]
        taken = [0, 0, 0]
        spent = [0.0, 0.0, 0.0]
        unit = -1
        while any(taken[n] < len(q) for n, q in enumerate(queues)):
            open_ = [n for n, q in enumerate(queues) if taken[n] < len(q)]
            now = free["pe"]
            late = {n: max(0.0, ready(queues[n][taken[n]]) - now) for n in open_}
            blocked = [n for n in open_ if queues[n][taken[n]][0] == "OT" and
                       ("O", *group(s - 1), 1) not in events and s == 0 or
                       queues[n][taken[n]][0] == "OT" and s == NG - 1 and ("O", 0, s, 0) not in events]
            open_ = [n for n in open_ if n not in blocked] or open_
            n = min(open_, key=lambda n: (late[n] > LATE and late[n], spent[n] / totals[n]))
            e = queues[n][taken[n]]
            if e[0] == "S" and e[3] != unit:
                unit = e[3]
                events += at_unit(s, unit)
            place(e)
            events.append(e)
            spent[n] += weights[n][taken[n]]
            taken[n] += 1
        return events

    for s in range(NG):
        stage(s)
    body = [e for s in range(NG) for e in stage(s)]

    prologue = [("STAT", 1, 0), ("AGGR", 1, 0), ("CLEAR", 1, 0), ("NORM", 1, 0), ("XT", 1, 0), ("FOLD", 1),
                ("STAT", 1, 1), ("AGGR", 1, 1), ("NORM", 1, 1), ("QK", 1, 0), ("V", 1, 0), ("XT", 1, 1),
                ("CLEAR", 1, 1), ("QK", 1, 1), ("V", 1, 1)]
    prologue += [("SAVE", 1, 0), ("SAVE", 1, 1), ("LK", 1, 0), ("LQ", 1, 0, 0), ("LQ", 1, 0, 1), ("LQ", 1, 1, 0)]
    prologue += [("LK", 1, g) for g in range(1, NG - 1)] + [("VA", 1, g) for g in range(NG - 1)]
    prologue += [("max", 1, 0, n) for n in range(first_half)]
    prologue += [("MM", 1, 0, 0), ("MT", 1, 0, 0), ("NM", 1, 0, 0)]
    prologue += [("max", 1, 0, n) for n in range(first_half, NM)] + [("MM", 1, 0, 1)]
    epilogue = [("PV", 0, NG - 1, NE - 1), ("O", 0, NG - 1, 1)]
    epilogue += [(kind, 0, q) for kind in ("OT", "AT", "WO") for q in (2, 3)]
    sections = [prologue, [e for e in body if e[1] >= 0], body, [e for e in body if e[1] <= 0] + epilogue]

    n, out = 0, []
    for at, section in enumerate(sections):
        uses = [e for e in section if e[0] in ring]
        if at == 2:
            assert len(uses) % 2 == 0
        before = [] if at == 0 else [(e[0], e[1] - 1, *e[2:]) for e in sections[at - 1] if e[0] in ring][-2:]
        known, placed = before + uses, []
        shift = len(before)
        for e in section:
            slot = held_by = None
            if e[0] in ring:
                slot = n % 2
                if shift >= 2:
                    held_by = known[shift - 2]
                n += 1
                shift += 1
            placed.append((e, slot, held_by))
        out.append(placed)
    return exp_units, exp_calls, max_units, out


def attention_stage(nc, ctx, g_, wq, wk, wv, wo, head_dirs, scale, B):
    x = g_.x
    C = wv.shape[0]
    KC = C // P
    H = head_dirs.shape[0]
    HD = C // H
    NG = H // HPG
    T = x.shape[1]
    NT = T // B
    SEQ = NT * P
    NTC = SEQ // CHUNK
    QKW = H * HD3
    K0 = 64
    exp_units, exp_calls, max_units, sections = attention_plan(NT, NG)
    NE, NC, NM = len(exp_units), len(exp_calls), len(max_units)
    first_half = len([1 for i, _ in max_units if i < TPC])

    def sb(name, shape, dt):
        return ctx.enter_context(nc.sbuf_tensor(f"at_{name}", shape, dt))

    def sem(name):
        return ctx.enter_context(nc.semaphore(f"at_{name}"))

    w_qk = sb("w_qk", [P, KC, P], F32)
    w_v = sb("w_v", [P, KC, C], F32)
    w_o = sb("w_o", [P, KC, C], F32)
    ident_bf = sb("ident_bf", [P, P], BF16)
    ident_r = sb("ident_r", [P, P], F32R)
    future = sb("future", [P, P], BF16)
    past = sb("past", [P, P], BF16)
    q_rows = sb("q_rows", [P, 2, HPG, SEQ], F32R)
    k_rows = sb("k_rows", [P, NG, SEQ], F32R)
    q_dram = nc.dram_tensor("q_rows_dram", [B, H, ROW_MAX + 2, SEQ], F32).ap()
    k_dram = nc.dram_tensor("k_rows_dram", [B, H, ROW_MAX, SEQ], F32).ap()
    v_aug = sb("v_aug", [P, NT, H, 2 * HD], F32)
    neg_max = sb("neg_max", [P, TPC, P], F32)

    dirs = sb("dirs", [P, QKW], F32)
    scale_b = sb("scale", [P, 1], F32)
    wk_sb = sb("wk", [P, KC, QKW], F32)
    on_dir = sb("on_dir", [P, KC, QKW], F32)
    on_dir_sum = sb("on_dir_sum", [P, KC, H], F32)
    along = sb("along", [P, KC, QKW], F32)
    qk_cleared, masks_cleared, loaded, v_loaded, o_loaded, fold = (
        sem(n) for n in ("qk_cleared", "masks_cleared", "loaded", "v_loaded", "o_loaded", "fold"))
    even_q_cleared, odd_q_cleared, k_cleared, v_cleared, neg_max_cleared, masks_done, zeroed = (
        sem(n) for n in ("even_q_cleared", "odd_q_cleared", "k_cleared", "v_cleared", "neg_max_cleared",
                         "masks_done", "zeroed"))

    probs = sb("probs", [P, 3, HPG, CHUNK], F32)
    qk_hi = sb("qk_hi", [P, SEQ], F32R)
    qk_lo = sb("qk_lo", [P, SEQ], F32R)
    xn = sb("xn", [P, TPC, C], F32)
    xn_t = sb("xn_t", [P, KC, CHUNK], F32)
    max_t = sb("max_t", [P, NTC, CHUNK], F32)
    v_sb = sb("v_sb", [P, NT, C], F32)
    o_t = sb("o_t", [P, NG, SEQ], F32)
    o_n = [xn[:, 2 * p:2 * p + 2, :] for p in range(2)]
    o_n_t = [xn_t[:, :, 2 * p * P:2 * (p + 1) * P] for p in range(2)]
    maxima = sb("maxima", [P, NT, HPG], F32)
    inv_sum = sb("inv_sum", [P, 2, H], F32)
    stats = sb("stats", [P, TPC, 6], F32)
    mv = sb("mv", [P, TPC, 2], F32)
    var_eps = sb("var_eps", [P, TPC], F32)
    rstd = sb("rstd", [P, TPC], F32)
    pairs = ctx.enter_context(nc.psum_tensor("at_pairs", [P, 2, 2, CHUNK], F32))
    s_t = ctx.enter_context(nc.psum_tensor("at_s_t", [P, 3, CHUNK], F32))
    o_ps = ctx.enter_context(nc.psum_tensor("at_o_ps", [P, CHUNK], F32))

    stats_done, mv_done, vareps_done, rstd_done, xn_done = (
        sem(n) for n in ("stats_done", "mv_done", "vareps_done", "rstd_done", "xn_done"))
    xt_ready, xt_copied = sem("xt_ready"), sem("xt_copied")
    qk_ready, qk_hi_done, qk_lo_done = sem("qk_ready"), sem("qk_hi_done"), sem("qk_lo_done")
    v_ready, v_copied, v_placed = sem("v_ready"), sem("v_copied"), sem("v_placed")
    q_saved, k_saved = sem("q_saved"), sem("k_saved")
    k_loaded = [sem(f"k_loaded{g}") for g in range(NG)]
    q_loaded = [[sem(f"q_loaded{parity}_{c}") for c in range(NTC)] for parity in range(2)]
    maxima_loaded = [sem(f"maxima_loaded{c}") for c in range(NTC)]
    scores_ready, max_done = sem("scores_ready"), sem("max_done")
    neg_hi_done, neg_max_done = sem("neg_hi_done"), sem("neg_max_done")
    mt_ready, max_t_done = sem("mt_ready"), sem("max_t_done")
    st_ready, exp_done, pv_done, o_done = (
        sem(n) for n in ("st_ready", "exp_done", "pv_done", "o_done"))
    ot_ready, inv_done, on_done = sem("ot_ready"), sem("inv_done"), sem("on_done")
    ont_ready, ont_copied = sem("ont_ready"), sem("ont_copied")
    wo_ready, x_done = sem("wo_ready"), sem("x_done")
    SAVES = len(PARTS) * 16
    LOADS = HPG * 16

    def freed(e):
        kind, db = e[0], e[1]
        if kind == "max":
            return max_done, NG * NM, db * NG * NM + e[2] * NM + e[3] + 1
        if kind == "MT":
            return max_t_done, NG * NTC, db * NG * NTC + e[2] * NTC + e[3] + 1
        s, n = {"XT": (xt_copied, 2), "QK": (qk_lo_done, NTC), "V": (v_copied, 2), "OT": (on_done, 4),
                "AT": (ont_copied, 4), "WO": (x_done, 4)}[kind]
        return s, n, db * n + e[2] + 1

    block = ctx.enter_context(nc.Block())

    def run(eng, kinds, emit):
        def section(n, b, at):
            for e, slot, held_by in sections[n]:
                if e[0] in kinds:
                    emit(e, slot, held_by, b, at)

        section(0, -1, lambda per, c: c - per)
        section(1, 0, lambda per, c: c)
        with eng.Fori(1, B - 1) as b:
            bases = {}

            def at(per, c):
                assert per + c > 0, (per, c)
                if per not in bases:
                    bases[per] = eng.snap(b * per)
                return bases[per] + c

            section(2, b, at)
        section(3, B - 1, lambda per, c: (B - 1) * per + c)

    pool_waits, dve_waits, sp_waits = sem("pool_waits"), sem("dve_waits"), sem("sp_waits")

    def wait(eng, semaphore, value, passed=None):
        if not (isinstance(value, int) and value <= 0):
            w = eng.wait_ge(semaphore, value)
            if passed is not None:
                w.then_inc(passed, 1)

    def tokens_made(per, db, at):
        n = at(per, (db + 2) * per)
        return min(n, B * per) if isinstance(n, int) else n

    def heads_per_bank(i, js):
        return max(1, min(len(js), CHUNK // ((i + 1) * P)))

    def repeated(mask, n):
        return mask[:, :].rearrange("p (o n) -> p o n", o=1).broadcast_to([P, n, P])

    def calls(db, g, u, j=0):
        return (db * NG + g) * NC + len([1 for v, js in exp_calls if (v, js[0]) < (u, j)])

    def bank_of(g, u, js):
        n = calls(0, g, u, js[0])
        return n % 3, n - 3 if n >= 3 else max(m for m in range(GC) if m % 3 == n) - GC

    GE, GC, GM = NG * NE, NG * NC, NG * NM

    @block.sync
    def _(sp):
        def emit(e, slot, held_by, b, at):
            kind, db = e[0], e[1]
            if kind == "SAVE":
                wait(sp, qk_lo_done, at(NTC, (db + 1) * NTC), sp_waits)
                dram, p0, saved = ((q_dram, 0, q_saved), (k_dram, K0, k_saved))[e[2]]
                for n, parts in enumerate(PARTS):
                    rows = dram[bass.ds(b + db, 1), :, n * HD3:(n + 1) * HD3, :]
                    sp.dma_start(rows.rearrange("o h d t -> (o h) d t"),
                                 (qk_hi, qk_lo)[parts[e[2]]][p0:p0 + QKW, :].bitcast(F32)).then_inc(saved, 16)
            elif kind == "LK":
                g = e[2]
                wait(sp, k_saved, at(SAVES, (db + 1) * SAVES), sp_waits)
                wait(sp, st_ready, at(GC, calls(db - 1, g + 1, 0)), sp_waits)
                for j in range(HPG):
                    sp.dma_start(k_rows[ROWS * j:ROWS * j + ROW_MAX, g, :].bitcast(F32),
                                 k_dram[bass.ds(b + db, 1), g * HPG + j, :, :].rearrange("o r t -> (o r) t")
                                 ).then_inc(k_loaded[g], 16)
            elif kind == "LQ":
                _, _, g, c = e
                s = slice(c * CHUNK, (c + 1) * CHUNK)
                wait(sp, q_saved, at(SAVES, (db + 1) * SAVES), sp_waits)
                wait(sp, st_ready, at(GC, calls(db, g - 2, TPC if c == 0 else NE)), sp_waits)
                for j in range(HPG):
                    sp.dma_start(q_rows[ROWS * j:ROWS * j + ROW_MAX + 2, g % 2, j, s].bitcast(F32),
                                 q_dram[bass.ds(b + db, 1), g * HPG + j, :, s].rearrange("o r t -> (o r) t")
                                 ).then_inc(q_loaded[g % 2][c], 16)
            else:
                _, _, g, c = e
                wait(sp, max_t_done, at(NG * NTC, (db * NG + g) * NTC + c + 1), sp_waits)
                for j in range(HPG):
                    r = slice(ROWS * j + ROW_MAX, ROWS * j + ROW_MAX + 2)
                    sp.dma_start(q_rows[r, g % 2, j, c * CHUNK:(c + 1) * CHUNK].bitcast(F32),
                                 max_t[r, c, :]).then_inc(maxima_loaded[c], 16)

        sp.dma_start(dirs[:, :], head_dirs.rearrange("h d -> (h d)").rearrange("(o n) -> o n", o=1)
                     .broadcast_to([P, QKW])).then_inc(loaded, 16)
        sp.dma_start(scale_b[:, :], scale.rearrange("(o n) -> o n", o=1).broadcast_to([P, 1])).then_inc(loaded, 16)
        sp.dma_start(wk_sb[:, :, :], wk.rearrange("(k p) n -> p k n", p=P)).then_inc(loaded, 16)
        sp.wait_ge(qk_cleared, 1)
        sp.dma_start(w_qk[:, :, 0:QKW], wq.rearrange("(k p) n -> p k n", p=P)).then_inc(loaded, 16)
        sp.dma_start(w_v[:, :, :], wv.rearrange("(k p) n -> p k n", p=P)).then_inc(v_loaded, 16)
        sp.dma_start(w_o[:, :, :], wo.rearrange("(k p) n -> p k n", p=P)).then_inc(o_loaded, 16)
        sp.wait_ge(even_q_cleared, 1)
        for b in range(B):
            sp.dma_start(q_dram[b, :, ROW_MAX:ROW_MAX + 2, :],
                         q_rows[0:H, 0, 0:2, :].bitcast(F32)).then_inc(zeroed, 16)
        sp.wait_ge(k_cleared, 1)
        sp.wait_ge(odd_q_cleared, 1)
        sp.wait_ge(zeroed, B * 16)
        run(sp, ("SAVE", "LK", "LQ", "NM"), emit)

    @block.gpsimd
    def _(pool):
        def emit(e, slot, held_by, b, at):
            kind, db = e[0], e[1]
            if kind == "AGGR":
                n = db * 2 + e[2]
                wait(pool, mv_done, at(2, n + 1))
                nc.gpsimd.tensor_tensor(var_eps[:, :], mv[:, :, 1], g_.eps[:, 0:TPC],
                                        ALU.add).then_inc(vareps_done, 1)
                wait(pool, vareps_done, at(2, n + 1))
                nc.gpsimd.tensor_tensor(rstd[:, :], var_eps[:, :], g_.neg_half[:, 0:TPC],
                                        ALU.pow).then_inc(rstd_done, 1)
            elif kind == "CLEAR":
                h = e[2]
                if h == 0:
                    nc.gpsimd.memset(neg_max[:], 0.0).then_inc(neg_max_cleared, 1)
                    nc.gpsimd.memset(q_rows[:, 0].bitcast(F32), 0.0).then_inc(even_q_cleared, 1)
                else:
                    nc.gpsimd.memset(k_rows[:].bitcast(F32), 1.0).then_inc(k_cleared, 1)
                    nc.gpsimd.memset(v_aug[:], 1.0).then_inc(v_cleared, 1)
                    pool.wait_ge(v_cleared, 1)
            elif kind == "VA":
                g = e[2]
                wait(pool, v_copied, at(2, (db + 1) * 2))
                wait(pool, pv_done, at(GE, ((db - 1) * NG + g + 1) * NE), pool_waits)
                hs = slice(g * HPG, (g + 1) * HPG)
                nc.gpsimd.tensor_copy(
                    v_aug[:, :, hs, 0:HD],
                    v_sb[:, :, g * HPG * HD:(g + 1) * HPG * HD].rearrange("p i (h d) -> p i h d", d=HD),
                ).then_inc(v_placed, 1)

        nc.gpsimd.memset(future[:], 0.0).then_inc(masks_cleared, 1)
        nc.gpsimd.memset(past[:], 0.0).then_inc(masks_cleared, 1)
        pool.wait_ge(masks_cleared, 2)
        nc.gpsimd.affine_select(out=future[:], in_=future[:], compare_op=ALU.is_ge, fill=MASKED,
                                base=0, pattern=[[-1, P]], channel_multiplier=1).then_inc(masks_done, 1)
        nc.gpsimd.affine_select(out=past[:], in_=past[:], compare_op=ALU.is_ge, fill=MASKED,
                                base=0, pattern=[[1, P]], channel_multiplier=-1).then_inc(masks_done, 1)
        run(pool, ("AGGR", "CLEAR", "VA"), emit)

    @block.scalar
    def _(act):
        def emit(e, slot, held_by, b, at):
            kind, db = e[0], e[1]
            if kind == "S":
                _, _, g, u, js = e
                tc, k, off, n = exp_units[u]
                if js[0] == 0:
                    wait(act, pv_done, at(GE, (db * NG + g) * NE + u - 2))
                n_call = calls(db, g, u, js[0])
                bank, _ = bank_of(g, u, js)
                wait(act, st_ready, at(GC, n_call + 1))
                nc.scalar.activation(probs[:, u % 3, js[0]:js[-1] + 1, 0:n],
                                     s_t[:, bank, 0:len(js) * n].rearrange("p (j n) -> p j n", n=n),
                                     ACT.Exp).then_inc(exp_done, 1)
            elif kind == "O":
                _, _, g, tc = e
                wait(act, pv_done, at(GE, (db * NG + g) * NE + (TPC if tc == 0 else NE)))
                own = 2 if (g, tc) == (NG - 1, NTC - 1) else 2 * tc - 2
                wait(act, ot_ready, at(4, db * 4 + own))
                nc.scalar.copy(o_t[:, g, tc * CHUNK:(tc + 1) * CHUNK], o_ps[:, :]).then_inc(o_done, 1)
            elif kind == "XT":
                h = e[2]
                wait(act, xt_ready, at(2, db * 2 + h + 1))
                wait(act, v_ready, at(2, db * 2 + h))
                wait(act, qk_ready, at(NTC, db * NTC + h))
                wait(act, wo_ready, at(4, (db - 1) * 4))
                nc.scalar.copy(xn_t[:, :, :], pairs[:, slot, :, :]).then_inc(xt_copied, 1)
            elif kind == "QK":
                tc = e[2]
                wait(act, qk_ready, at(NTC, db * NTC + tc + 1))
                wait(act, q_saved, at(SAVES, db * SAVES))
                wait(act, k_saved, at(SAVES, db * SAVES))
                nc.scalar.copy(qk_hi[:, tc * CHUNK:(tc + 1) * CHUNK], pairs[:, slot, 0, :]).then_inc(qk_hi_done, 1)
            elif kind == "V":
                h = e[2]
                wait(act, v_ready, at(2, db * 2 + h + 1))
                wait(act, v_placed, at(NG, db * NG))
                nc.scalar.copy(v_sb[:, h * TPC:(h + 1) * TPC, :],
                               pairs[:, slot, :, :].rearrange("p a (b c) -> p (a b) c", c=C)).then_inc(v_copied, 1)
            else:
                q = e[2]
                wait(act, ont_ready, at(4, db * 4 + q + 1))
                wait(act, wo_ready, at(4, db * 4 + q - 1))
                wait(act, v_ready, tokens_made(2, db, at))
                wait(act, qk_ready, tokens_made(NTC, db, at))
                nc.scalar.copy(o_n_t[q % 2],
                               pairs[:, slot, 0, :].rearrange("p (k t) -> p k t", k=KC)).then_inc(ont_copied, 1)

        run(act, ("S", "O", "XT", "QK", "V", "AT"), emit)

    @block.vector
    def _(dve):
        def token_tile(b, db, i):
            return x[:, bass.ds((b + db) * NT + i, 1), :].rearrange("p a c -> p (a c)")

        def emit(e, slot, held_by, b, at):
            kind, db = e[0], e[1]
            if kind == "FOLD":
                dve.wait_ge(loaded, 4 * 16)
                dirs_b = dirs[:, :].rearrange("p (o n) -> p o n", o=1).broadcast_to([P, KC, QKW])
                nc.vector.tensor_tensor(on_dir[:], wk_sb[:], dirs_b, ALU.mult).then_inc(fold, 1)
                dve.wait_ge(fold, 1)
                nc.vector.tensor_reduce(on_dir_sum[:], on_dir[:].rearrange("p k (h d) -> p k h d", d=HD3),
                                        AX_X, ALU.add).then_inc(fold, 1)
                dve.wait_ge(fold, 2)
                for d in range(HD3):
                    last = nc.vector.tensor_tensor(
                        along[:].rearrange("p k (h d) -> p k h d", d=HD3)[:, :, :, d], on_dir_sum[:],
                        dirs_b.rearrange("p k (h d) -> p k h d", d=HD3)[:, :, :, d], ALU.mult)
                last.then_inc(fold, 1)
                dve.wait_ge(fold, 3)
                nc.vector.scalar_tensor_tensor(out=w_qk[:, :, K0:K0 + QKW], in0=wk_sb[:], scalar=scale_b[:, 0:1],
                                               in1=along[:], op0=ALU.mult, op1=ALU.add).then_inc(fold, 1)
                nc.vector.tensor_copy(ident_bf[:], g_.ident[:]).then_inc(fold, 1)
                nc.vector.tensor_copy(ident_r[:], g_.ident[:]).then_inc(fold, 1)
            elif kind == "CLEAR":
                if e[2]:
                    nc.vector.memset(q_rows[:, 1].bitcast(F32), 0.0).then_inc(odd_q_cleared, 1)
                    dve.wait_ge(neg_max_cleared, 1)
            elif kind == "STAT":
                h = e[2]
                for i in range(TPC):
                    last = nc.vector.bn_stats(stats[:, i, :], token_tile(b, db, h * TPC + i))
                last.then_inc(stats_done, 1)
            elif kind == "AGGR":
                n = db * 2 + e[2]
                wait(dve, xn_done, at(2, n))
                wait(dve, stats_done, at(2, n + 1), dve_waits)
                for i in range(TPC):
                    last = nc.vector.bn_aggr(mv[:, i, :], stats[:, i, :])
                last.then_inc(mv_done, 1)
            elif kind == "NORM":
                h = e[2]
                n = db * 2 + h
                wait(dve, rstd_done, at(2, n + 1))
                wait(dve, xt_ready, at(2, n))
                wait(dve, ont_ready, at(4, (db - 1) * 4))
                for i in range(TPC):
                    last = nc.vector.tensor_scalar(xn[:, i, :], token_tile(b, db, h * TPC + i), mv[:, i, 0:1],
                                                   rstd[:, i:i + 1], ALU.subtract, ALU.mult)
                last.then_inc(xn_done, 1)
            elif kind == "QK":
                tc = e[2]
                wait(dve, qk_hi_done, at(NTC, db * NTC + tc + 1))
                wait(dve, q_saved, at(SAVES, db * SAVES))
                wait(dve, k_saved, at(SAVES, db * SAVES))
                s = slice(tc * CHUNK, (tc + 1) * CHUNK)
                nc.vector.tensor_tensor(qk_lo[:, s], pairs[:, slot, 0, :], qk_hi[:, s],
                                        ALU.subtract).then_inc(qk_lo_done, 1)
            elif kind == "max":
                _, _, g, m = e
                i, js = max_units[m]
                n = (i + 1) * P
                wait(dve, scores_ready, at(GM, (db * NG + g) * NM + m + 1))
                if m in (0, first_half):
                    wait(dve, neg_max_done, at(NG * NTC, (db * NG + g) * NTC - 1 + (m > 0)))
                if n <= CHUNK:
                    share = heads_per_bank(i, js)
                    nc.vector.tensor_reduce(
                        maxima[:, i, js[0]:js[-1] + 1].rearrange("p (a j) -> p a j", j=share),
                        pairs[:, slot, 0:len(js) // share, 0:share * n].rearrange("p a (j n) -> p a j n", n=n),
                        AX_X, ALU.max).then_inc(max_done, 1)
                else:
                    nc.vector.tensor_reduce(maxima[:, i, js[0]:js[0] + 1],
                                            pairs[:, slot, :, :].rearrange("p a n -> p (a n)")[:, 0:n], AX_X,
                                            ALU.max).then_inc(max_done, 1)
            elif kind == "MM":
                _, _, g, c = e
                n = (db * NG + g) * NTC + c
                rows = neg_max[:, :, :].rearrange("p i (j r) -> p i j r", r=ROWS)
                m = maxima[:, c * TPC:(c + 1) * TPC, :]
                wait(dve, max_done, at(GM, (db * NG + g) * NM + (first_half if c == 0 else NM)))
                wait(dve, mt_ready, at(NG * NTC, n))
                nc.vector.tensor_scalar(rows[:, :, :, ROW_MAX].bitcast(F32R), m, -1.0, None,
                                        ALU.mult).then_inc(neg_hi_done, 1)
                wait(dve, neg_hi_done, at(NG * NTC, n + 1))
                nc.vector.scalar_tensor_tensor(out=rows[:, :, :, ROW_MAX + 1].bitcast(F32R), in0=m, scalar=-1.0,
                                               in1=rows[:, :, :, ROW_MAX], op0=ALU.mult,
                                               op1=ALU.subtract).then_inc(neg_max_done, 1)
            elif kind == "MT":
                _, _, g, c = e
                n = (db * NG + g) * NTC + c
                wait(dve, mt_ready, at(NG * NTC, n + 1))
                wait(dve, maxima_loaded[c], at(NG * LOADS, (db * NG + g) * LOADS))
                nc.vector.tensor_copy(max_t[:, c, :], pairs[:, slot, 0, :]).then_inc(max_t_done, 1)
            elif kind == "OT":
                q = e[2]
                n = db * 4 + q
                heads = pairs[:, slot, :, :].rearrange("p a (h r) -> p a h r", r=2 * HD)
                wait(dve, ot_ready, at(4, n + 1))
                wait(dve, on_done, at(4, n))
                nc.vector.reciprocal(inv_sum[:, :, :], heads[:, :, :, HD]).then_inc(inv_done, 1)
                wait(dve, inv_done, at(4, n + 1))
                wait(dve, ont_ready, at(4, n - 1))
                wait(dve, xt_ready, tokens_made(2, db, at))
                nc.vector.tensor_tensor(
                    o_n[q % 2].rearrange("p a (h d) -> p a h d", d=HD), heads[:, :, :, 0:HD],
                    inv_sum[:, :, :].rearrange("p a (h o) -> p a h o", o=1).broadcast_to([P, 2, H, HD]),
                    ALU.mult).then_inc(on_done, 1)
            else:
                q = e[2]
                wait(dve, wo_ready, at(4, db * 4 + q + 1))
                two = x[:, bass.ds((b + db) * NT + 2 * q, 2), :]
                nc.vector.tensor_tensor(two, pairs[:, slot, 0, :].rearrange("p (a c) -> p a c", c=C), two,
                                        ALU.add).then_inc(x_done, 1)

        nc.vector.memset(w_qk[:], 0.0).then_inc(qk_cleared, 1)
        run(dve, ("STAT", "AGGR", "NORM", "FOLD", "CLEAR", "QK", "max", "MM", "MT", "OT", "WO"), emit)

    @block.tensor
    def _(pe):
        def emit(e, slot, held_by, b, at):
            kind, db = e[0], e[1]
            if held_by is not None:
                semaphore, per, count = freed(held_by)
                wait(pe, semaphore, at(per, count))
            if kind == "FOLD":
                pe.wait_ge(fold, 6)
                pe.wait_ge(loaded, 4 * 16)
                pe.wait_ge(v_loaded, 16)
                pe.wait_ge(o_loaded, 16)
                pe.wait_ge(masks_done, 2)
            elif kind == "S":
                _, _, g, u, js = e
                tc, k, off, n = exp_units[u]
                if js[0] == 0 and u in (0, TPC):
                    wait(pe, maxima_loaded[tc], at(NG * LOADS, (db * NG + g + 1) * LOADS))
                diagonal = k >= tc * TPC
                bank, before = bank_of(g, u, js)
                wait(pe, exp_done, at(GC, db * GC + before + 1))
                for a, j in enumerate(js):
                    last = nc.tensor.matmul(s_t[:, bank, a * n:(a + 1) * n], k_rows[:, g, k * P:(k + 1) * P],
                                            q_rows[:, g % 2, j, tc * CHUNK + off:(tc + 1) * CHUNK],
                                            start=(a == 0), stop=not diagonal and a == len(js) - 1)
                if diagonal:
                    scores = s_t[:, bank, 0:len(js) * n].rearrange("p (j n) -> p j n", n=n)[:, :, 0:P]
                    last = nc.tensor.matmul(scores, ident_bf[:, :], repeated(past, len(js)),
                                            start=False, stop=True)
                last.then_inc(st_ready, 1)
            elif kind == "PV":
                _, _, g, u = e
                tc, k, off, n = exp_units[u]
                if u == 0:
                    wait(pe, v_placed, at(NG, db * NG + g + 1))
                if k == 0:
                    wait(pe, o_done, at(NG * 2, (db * NG + g) * 2 + tc))
                wait(pe, exp_done, at(GC, calls(db, g, u + 1)))
                for j in range(HPG):
                    last = nc.tensor.matmul(o_ps[ROWS * j:ROWS * (j + 1), off:off + n],
                                            v_aug[:, k, g * HPG + j, :], probs[:, u % 3, j, 0:n],
                                            start=(k == 0), stop=(k == (tc + 1) * TPC - 1))
                last.then_inc(pv_done, 1)
            elif kind == "max":
                _, _, g, m = e
                i, js = max_units[m]
                n = (i + 1) * P
                if m == 0:
                    wait(pe, k_loaded[g], at(LOADS, (db + 1) * LOADS))
                if m in (0, first_half):
                    c = int(m > 0)
                    wait(pe, q_loaded[g % 2][c], at(NG // 2 * LOADS, (db * (NG // 2) + g // 2 + 1) * LOADS))
                share = heads_per_bank(i, js)
                for a, j in enumerate(js):
                    for c0 in range(0, n, CHUNK):
                        c1, o = min(n, c0 + CHUNK), a % share * n
                        nc.tensor.matmul(pairs[:, slot, a // share + c0 // CHUNK, o:o + c1 - c0],
                                         q_rows[:, g % 2, j, i * P:(i + 1) * P], k_rows[:, g, c0:c1],
                                         start=(a % share == 0), stop=(c1 < n))
                for a in range(0, len(js), share):
                    bank, end = a // share + (n - 1) // CHUNK, (n - 1) % CHUNK + 1
                    scores = pairs[:, slot, bank, 0:share * end].rearrange("p (j n) -> p j n", n=end)
                    last = nc.tensor.matmul(scores[:, :, end - P:end], ident_bf[:, :], repeated(future, share),
                                            start=False, stop=True)
                last.then_inc(scores_ready, 1)
            elif kind == "MT":
                _, _, g, c = e
                wait(pe, neg_max_done, at(NG * NTC, (db * NG + g) * NTC + c + 1))
                for i in range(TPC):
                    last = nc.tensor.matmul(pairs[:, slot, 0, i * P:(i + 1) * P], neg_max[:, i, :].bitcast(F32R),
                                            ident_r[:, :], start=True, stop=True)
                last.then_inc(mt_ready, 1)
            elif kind == "XT":
                h = e[2]
                wait(pe, xn_done, at(2, db * 2 + h + 1))
                for kc in range(KC):
                    for i in range(TPC):
                        last = nc.tensor.transpose(pairs[:, slot, kc, i * P:(i + 1) * P],
                                                   xn[:, i, kc * P:(kc + 1) * P], g_.ident[:, :])
                last.then_inc(xt_ready, 1)
            elif kind == "QK":
                tc = e[2]
                wait(pe, xt_copied, at(2, db * 2 + tc + 1))
                for kc in range(KC):
                    last = nc.tensor.matmul(pairs[:, slot, 0, :], w_qk[:, kc, :],
                                            xn_t[:, kc, :],
                                            start=(kc == 0), stop=(kc == KC - 1))
                last.then_inc(qk_ready, 1)
            elif kind == "V":
                h = e[2]
                wait(pe, xt_copied, at(2, db * 2 + h + 1))
                for i in range(TPC):
                    t = i * P
                    for kc in range(KC):
                        last = nc.tensor.matmul(pairs[:, slot, i // 2, i % 2 * C:(i % 2 + 1) * C],
                                                xn_t[:, kc, t:t + P], w_v[:, kc, :],
                                                start=(kc == 0), stop=(kc == KC - 1))
                last.then_inc(v_ready, 1)
            elif kind == "OT":
                q = e[2]
                wait(pe, o_done, at(NG * 2, (db * NG + NG - 1) * 2 + q // 2 + 1))
                for a in range(2):
                    for g in range(NG):
                        t = (2 * q + a) * P
                        last = nc.tensor.transpose(pairs[:, slot, a, g * P:(g + 1) * P], o_t[:, g, t:t + P],
                                                   g_.ident[:, :])
                last.then_inc(ot_ready, 1)
            elif kind == "AT":
                q = e[2]
                wait(pe, on_done, at(4, db * 4 + q + 1))
                for kc in range(KC):
                    for a in range(2):
                        t = (kc * 2 + a) * P
                        last = nc.tensor.transpose(pairs[:, slot, 0, t:t + P], o_n[q % 2][:, a, kc * P:(kc + 1) * P],
                                                   g_.ident[:, :])
                last.then_inc(ont_ready, 1)
            else:
                q = e[2]
                wait(pe, ont_copied, at(4, db * 4 + q + 1))
                for a in range(2):
                    for kc in range(KC):
                        last = nc.tensor.matmul(pairs[:, slot, 0, a * C:(a + 1) * C], o_n_t[q % 2][:, kc, a * P:(a + 1) * P],
                                                w_o[:, kc, :], start=(kc == 0), stop=(kc == KC - 1))
                last.then_inc(wo_ready, 1)

        run(pe, ("FOLD", "S", "PV", "max", "MT", "XT", "QK", "V", "OT", "AT", "WO"), emit)


def macaron(nc, x_in, wq, wk, wv, wo, head_dirs, scale, w_gate, w_up, w_down, out):
    B, SEQ, C = x_in.shape
    T = B * SEQ // P
    x_tiles = x_in.rearrange("b (i p) c -> p (b i) c", p=P)
    out_tiles = out.rearrange("b (i p) c -> p (b i) c", p=P)
    with ExitStack() as ctx:
        g = Buffers()
        g.x = ctx.enter_context(nc.sbuf_tensor("x", [P, T, C], F32))
        g.ident = ctx.enter_context(nc.sbuf_tensor("ident", [P, P], F32))
        g.ones = ctx.enter_context(nc.sbuf_tensor("ones", [P, 1], F32))
        g.neg_half = ctx.enter_context(nc.sbuf_tensor("neg_half", [P, 8], F32))
        g.eps = ctx.enter_context(nc.sbuf_tensor("eps", [P, 8], F32))
        g.flag = ctx.enter_context(nc.sbuf_tensor("flag", [1, 1], I32))
        g.flag_done = ctx.enter_context(nc.semaphore("flag_done"))
        g.consts_done = ctx.enter_context(nc.semaphore("consts_done"))
        g.N_CONSTS = 5
        with ExitStack() as consts:
            block = consts.enter_context(nc.Block())

            @block.gpsimd
            def _(pool):
                nc.gpsimd.memset(g.ones[:], 1.0).then_inc(g.consts_done, 1)
                nc.gpsimd.memset(g.neg_half[:], -0.5).then_inc(g.consts_done, 1)
                nc.gpsimd.memset(g.ident[:], 0.0).then_inc(g.consts_done, 1)
                nc.gpsimd.memset(g.eps[:], EPS).then_inc(g.consts_done, 1)
                pool.wait_ge(g.consts_done, 4)
                nc.gpsimd.affine_select(out=g.ident[:], in_=g.ident[:], compare_op=ALU.not_equal, fill=1.0,
                                        base=0, pattern=[[-1, P]], channel_multiplier=1).then_inc(g.consts_done, 1)
        with ExitStack() as stage:
            ffn_stage(nc, stage, g, "ffn1", w_gate, w_up, w_down, x_tiles, None, find_flag=True)
        with ExitStack() as stage:
            attention_stage(nc, stage, g, wq, wk, wv, wo, head_dirs, scale, B)
        with ExitStack() as stage:
            ffn_stage(nc, stage, g, "ffn2", w_gate, w_up, w_down, None, out_tiles, find_flag=False)


def kernel(L0_attn_x, L0_attn_wq, L0_attn_wk, L0_attn_wv, L0_attn_wo, L0_attn_head_dirs, L0_attn_scale,
           L0_ffn_w_gate, L0_ffn_w_up, L0_ffn_w_down):
    import numpy as np
    import concourse.bacc as bacc
    from concourse.bass_utils import run_bass_kernel_spmd

    arrays = {
        "x_in": L0_attn_x, "wq": L0_attn_wq, "wk": L0_attn_wk, "wv": L0_attn_wv, "wo": L0_attn_wo,
        "head_dirs": L0_attn_head_dirs, "scale": L0_attn_scale,
        "w_gate": np.asarray(L0_ffn_w_gate).T, "w_up": np.asarray(L0_ffn_w_up).T,
        "w_down": np.asarray(L0_ffn_w_down).T,
    }
    arrays = {name: np.ascontiguousarray(a) for name, a in arrays.items()}
    nc = bacc.Bacc("TRN2", target_bir_lowering=False, num_devices=1)
    aps = [nc.dram_tensor(name, a.shape, mybir.dt.from_np(a.dtype), kind="ExternalInput").ap()
           for name, a in arrays.items()]
    out = nc.dram_tensor("out", arrays["x_in"].shape, F32, kind="ExternalOutput").ap()
    macaron(nc, *aps, out)
    result = run_bass_kernel_spmd(nc, [arrays], core_ids=[0])
    return result.results[0]["out"]
```
